# Optimizing a Trainium2 kernel written in Bass

```python
import numpy as np
import jax
import jax.numpy as jnp

def _softmax(x, axis=-1):
    return jax.nn.softmax(x, axis=axis)

def _gelu(x):
    return jax.nn.gelu(x, approximate=True)

def _silu(x):
    return jax.nn.silu(x)

def _sigmoid(x):
    return jax.nn.sigmoid(x)

def _layernorm(x, axis=-1, eps=1e-05):
    m = jnp.mean(x, axis=axis, keepdims=True)
    v = jnp.var(x, axis=axis, keepdims=True)
    return (x - m) / jnp.sqrt(v + eps)

def _scatter_add(tgt, idx, src, axis=0):
    return tgt.at[idx].add(src)

def _segment_sum(src, seg, n):
    return jax.ops.segment_sum(src, seg, n)
kernel_name = 'mk_adj_preln_d4_adj_r2_1e9c3c'

def setup_inputs(seed: int=0):
    np.random.seed(seed)
    _w = jnp.asarray

    def _rec_inputs():
        import jax
        import jax.numpy as jnp
        _gk = jax.random.key(seed)
        x = -0.0003929 + 0.9999 * jax.random.normal(jax.random.fold_in(_gk, 1), (64, 128, 128), jnp.float32)
        _w = (1.0 + jnp.arange(128, dtype=jnp.float32)) ** (-0.5)
        _w = _w / _w.mean()
        _pij = jnp.clip(0.125 * _w[:, None] * _w[None, :], 0.0, 1.0)
        _a = jax.random.uniform(jax.random.fold_in(_gk, 2), (128, 128)) < _pij
        _a = jnp.logical_or(_a, jnp.swapaxes(_a, -1, -2))
        _a = jnp.logical_or(_a, jnp.eye(128, dtype=bool))
        _af = _a.astype(jnp.float32)
        _d = jnp.maximum(_af.sum(-1), 1.0) ** (-0.5)
        _af = _af * _d[..., :, None] * _d[..., None, :]
        adj = _af
        return (x, adj)
    x, adj = _rec_inputs()

    def _L0_gnn_setup():
        import jax, jax.numpy as jnp
        import numpy as np
        B, N, D_IN, HID, D_OUT = (64, 512, 128, 128, 128)
        key = jax.random.key(seed)
        kf, ka, kw1, kw2 = jax.random.split(key, 4)
        features = jax.random.normal(kf, (B, N, D_IN), dtype=jnp.float32)
        A = jax.random.uniform(ka, (N, N), dtype=jnp.float32)
        A = 0.5 * (A + A.T)
        lim1 = float(np.sqrt(6.0 / (D_IN + HID)))
        lim2 = float(np.sqrt(6.0 / (HID + D_OUT)))
        W1 = jax.random.uniform(kw1, (D_IN, HID), minval=-lim1, maxval=lim1, dtype=jnp.float32)
        b1 = jnp.zeros((HID,), jnp.float32)
        W2 = jax.random.uniform(kw2, (HID, D_OUT), minval=-lim2, maxval=lim2, dtype=jnp.float32)
        b2 = jnp.zeros((D_OUT,), jnp.float32)
        return {'features': features, 'A': A, 'W1': W1, 'b1': b1, 'W2': W2, 'b2': b2}
    _L0_gnn_all = _L0_gnn_setup()
    _L0_gnn_in = {k: v for k, v in _L0_gnn_all.items() if k in ('W1', 'b1', 'W2', 'b2')}
    del _L0_gnn_all

    def _L1_gnn_setup():
        import jax, jax.numpy as jnp
        import numpy as np
        EPS = 1e-05

        def _batchnorm(x, gamma, beta):
            mu = jnp.mean(x, axis=0)
            var = jnp.var(x, axis=0)
            return (x - mu) * jax.lax.rsqrt(var + EPS) * gamma + beta
        key = jax.random.key(seed)
        ks = jax.random.split(key, 4)
        b, n, d, h, o = (32, 1024, 128, 256, 128)
        features = jax.random.normal(ks[0], (b, n, d), dtype=jnp.float32)
        A = jax.random.uniform(ks[1], (n, n), dtype=jnp.float32)
        lim1 = float(np.sqrt(6.0 / (d + h)))
        W1 = jax.random.uniform(ks[2], (h, d), minval=-lim1, maxval=lim1, dtype=jnp.float32)
        b1 = jnp.zeros((h,), jnp.float32)
        lim2 = float(np.sqrt(6.0 / (h + o)))
        W2 = jax.random.uniform(ks[3], (o, h), minval=-lim2, maxval=lim2, dtype=jnp.float32)
        b2 = jnp.zeros((o,), jnp.float32)
        g1 = jnp.ones((h,), jnp.float32)
        be1 = jnp.zeros((h,), jnp.float32)
        g2 = jnp.ones((o,), jnp.float32)
        be2 = jnp.zeros((o,), jnp.float32)
        return {'features': features, 'A': A, 'W1': W1, 'b1': b1, 'g1': g1, 'be1': be1, 'W2': W2, 'b2': b2, 'g2': g2, 'be2': be2}
    _L1_gnn_all = _L1_gnn_setup()
    _L1_gnn_in = {k: v for k, v in _L1_gnn_all.items() if k in ('W1', 'b1', 'g1', 'be1', 'W2', 'b2', 'g2', 'be2')}
    del _L1_gnn_all

    def _L2_gnn_setup():
        import jax, jax.numpy as jnp
        import numpy as np
        B, T, D, H = (64, 1024, 128, 128)
        MAX_SKIP = 4

        def _lstm_last(Wih, Whh, bih, bhh, xs):
            N, _, Hd = xs.shape
            bias = bih + bhh

            def step(carry, x_t):
                h, c = carry
                g = x_t @ Wih.T + h @ Whh.T + bias
                i, f, gg, o = jnp.split(g, 4, axis=-1)
                c = jax.nn.sigmoid(f) * c + jax.nn.sigmoid(i) * jnp.tanh(gg)
                h = jax.nn.sigmoid(o) * jnp.tanh(c)
                return ((h, c), None)
            init = (jnp.zeros((N, Hd), xs.dtype), jnp.zeros((N, Hd), xs.dtype))
            (h_last, _), _ = jax.lax.scan(step, init, jnp.swapaxes(xs, 0, 1))
            return h_last
        key = jax.random.key(seed)
        ks = jax.random.split(key, 8)
        s = 0.05
        x = jax.random.normal(ks[0], (B, T, D), jnp.float32)
        adj = jax.random.uniform(ks[1], (T, T), jnp.float32) / T
        Wg0 = jax.random.normal(ks[2], (D, H), jnp.float32) * s
        bg0 = jnp.zeros((H,), jnp.float32)
        Wg1 = jax.random.normal(ks[3], (H, H), jnp.float32) * s
        bg1 = jnp.zeros((H,), jnp.float32)
        Wih = jax.random.normal(ks[4], (MAX_SKIP, 4 * H, H), jnp.float32) * s
        Whh = jax.random.normal(ks[5], (MAX_SKIP, 4 * H, H), jnp.float32) * s
        bih = jax.random.normal(ks[6], (MAX_SKIP, 4 * H), jnp.float32) * s
        bhh = jax.random.normal(ks[7], (MAX_SKIP, 4 * H), jnp.float32) * s
        return dict(x=x, adj=adj, Wg0=Wg0, bg0=bg0, Wg1=Wg1, bg1=bg1, Wih=Wih, Whh=Whh, bih=bih, bhh=bhh)
    _L2_gnn_all = _L2_gnn_setup()
    _L2_gnn_in = {k: v for k, v in _L2_gnn_all.items() if k in ('Wg0', 'bg0', 'Wg1', 'bg1', 'Wih', 'Whh', 'bih', 'bhh')}
    del _L2_gnn_all

    def _L3_gnn_setup():
        import jax, jax.numpy as jnp
        import numpy as np
        B, N, IN_DIM, OUT_DIM, H = (2, 2048, 128, 128, 4)
        HEAD_DIM = OUT_DIM // H
        EDGE_P = 0.01
        key = jax.random.key(seed)
        k1, k2, k3 = jax.random.split(key, 3)
        h = jax.random.normal(k1, (B, N, IN_DIM), dtype=jnp.float32)
        W = jax.random.normal(k2, (IN_DIM, 3 * OUT_DIM), dtype=jnp.float32) / np.sqrt(IN_DIM)
        adj = (jax.random.uniform(k3, (N, N)) < EDGE_P).astype(jnp.float32)
        adj = jnp.maximum(adj, jnp.eye(N, dtype=jnp.float32))
        return {'h': h, 'W': W, 'adj': adj}
    _L3_gnn_all = _L3_gnn_setup()
    _L3_gnn_in = {k: v for k, v in _L3_gnn_all.items() if k in ('W',)}
    del _L3_gnn_all
    return {'x': x, 'adj': adj, 'L0_gnn_W1': _L0_gnn_in['W1'], 'L0_gnn_b1': _L0_gnn_in['b1'], 'L0_gnn_W2': _L0_gnn_in['W2'], 'L0_gnn_b2': _L0_gnn_in['b2'], 'L1_gnn_W1': _L1_gnn_in['W1'], 'L1_gnn_b1': _L1_gnn_in['b1'], 'L1_gnn_g1': _L1_gnn_in['g1'], 'L1_gnn_be1': _L1_gnn_in['be1'], 'L1_gnn_W2': _L1_gnn_in['W2'], 'L1_gnn_b2': _L1_gnn_in['b2'], 'L1_gnn_g2': _L1_gnn_in['g2'], 'L1_gnn_be2': _L1_gnn_in['be2'], 'L2_gnn_Wg0': _L2_gnn_in['Wg0'], 'L2_gnn_bg0': _L2_gnn_in['bg0'], 'L2_gnn_Wg1': _L2_gnn_in['Wg1'], 'L2_gnn_bg1': _L2_gnn_in['bg1'], 'L2_gnn_Wih': _L2_gnn_in['Wih'], 'L2_gnn_Whh': _L2_gnn_in['Whh'], 'L2_gnn_bih': _L2_gnn_in['bih'], 'L2_gnn_bhh': _L2_gnn_in['bhh'], 'L3_gnn_W': _L3_gnn_in['W']}

def reference(x, adj, L0_gnn_W1, L0_gnn_b1, L0_gnn_W2, L0_gnn_b2, L1_gnn_W1, L1_gnn_b1, L1_gnn_g1, L1_gnn_be1, L1_gnn_W2, L1_gnn_b2, L1_gnn_g2, L1_gnn_be2, L2_gnn_Wg0, L2_gnn_bg0, L2_gnn_Wg1, L2_gnn_bg1, L2_gnn_Wih, L2_gnn_Whh, L2_gnn_bih, L2_gnn_bhh, L3_gnn_W):
    import jax
    import jax.numpy as jnp

    def _L0_gnn_ref(features, A, W1, b1, W2, b2):
        import jax, jax.numpy as jnp
        import numpy as np
        B, N, D_IN, HID, D_OUT = (64, 512, 128, 128, 128)
        deg = jnp.sum(A, axis=0) + jnp.sum(A, axis=1) - jnp.diagonal(A)
        d_inv_sqrt = jnp.where(deg > 0, jax.lax.rsqrt(deg), 0.0)
        L = jnp.diag(deg) - A
        L_norm = d_inv_sqrt[:, None] * L * d_inv_sqrt[None, :]
        _, U = jnp.linalg.eigh(L_norm)
        agg = jnp.einsum('mn,bnd->bmd', U.T, features)
        h = jax.nn.relu(agg @ W1 + b1)
        out = h @ W2 + b2
        return jnp.einsum('nm,bmd->bnd', U, out)

    def _L1_gnn_ref(features, A, W1, b1, g1, be1, W2, b2, g2, be2):
        import jax, jax.numpy as jnp
        import numpy as np
        EPS = 1e-05

        def _batchnorm(x, gamma, beta):
            mu = jnp.mean(x, axis=0)
            var = jnp.var(x, axis=0)
            return (x - mu) * jax.lax.rsqrt(var + EPS) * gamma + beta
        b, n, d = features.shape
        A_norm = A + jnp.eye(n, dtype=A.dtype)
        deg = jnp.sum(A_norm, axis=0) + jnp.sum(A_norm, axis=1) - jnp.diagonal(A_norm)
        dinv = jax.lax.rsqrt(deg)
        A_hat = A_norm * dinv[:, None] * dinv[None, :]
        agg = jnp.einsum('nm,bmd->bnd', A_hat, features)
        x = agg.reshape(-1, d)
        h = jax.nn.relu(_batchnorm(x @ W1.T + b1, g1, be1))
        out = h @ W2.T + b2
        out = _batchnorm(out, g2, be2)
        return out.reshape(b, n, -1)

    def _L2_gnn_ref(x, adj, Wg0, bg0, Wg1, bg1, Wih, Whh, bih, bhh):
        import jax, jax.numpy as jnp
        import numpy as np
        B, T, D, H = (64, 1024, 128, 128)
        MAX_SKIP = 4

        def _lstm_last(Wih, Whh, bih, bhh, xs):
            N, _, Hd = xs.shape
            bias = bih + bhh

            def step(carry, x_t):
                h, c = carry
                g = x_t @ Wih.T + h @ Whh.T + bias
                i, f, gg, o = jnp.split(g, 4, axis=-1)
                c = jax.nn.sigmoid(f) * c + jax.nn.sigmoid(i) * jnp.tanh(gg)
                h = jax.nn.sigmoid(o) * jnp.tanh(c)
                return ((h, c), None)
            init = (jnp.zeros((N, Hd), xs.dtype), jnp.zeros((N, Hd), xs.dtype))
            (h_last, _), _ = jax.lax.scan(step, init, jnp.swapaxes(xs, 0, 1))
            return h_last
        h = jax.nn.relu(jnp.einsum('ts,bsh->bth', adj, x @ Wg0 + bg0))
        h = jax.nn.relu(jnp.einsum('ts,bsh->bth', adj, h @ Wg1 + bg1))
        Bv, Tv, Hd = h.shape
        for p in range(1, MAX_SKIP + 1):
            nw = Tv // p
            wins = h[:, :nw * p, :].reshape(Bv * nw, p, Hd)
            last = _lstm_last(Wih[p - 1], Whh[p - 1], bih[p - 1], bhh[p - 1], wins)
            idx = jnp.arange(nw) * p + (p - 1)
            h = h.at[:, idx, :].set(last.reshape(Bv, nw, Hd))
        return h

    def _L3_gnn_ref(h, W, adj):
        import jax, jax.numpy as jnp
        import numpy as np
        B, N, IN_DIM, OUT_DIM, H = (2, 2048, 128, 128, 4)
        HEAD_DIM = OUT_DIM // H
        EDGE_P = 0.01
        Bn, Nn, _ = h.shape
        qkv = h @ W
        qkv = qkv.reshape(Bn, Nn, 3, H, HEAD_DIM).transpose(2, 0, 3, 1, 4)
        q, k, v = (qkv[0], qkv[1], qkv[2])
        mask = jnp.where(adj == 0, -jnp.inf, 0.0)
        scores = jnp.einsum('bhid,bhjd->bhij', q, k) / np.sqrt(HEAD_DIM) + mask
        attn = jax.nn.softmax(scores, axis=-1)
        out = jnp.einsum('bhij,bhjd->bhid', attn, v)
        return out.transpose(0, 2, 1, 3).reshape(Bn, Nn, OUT_DIM)
    h = jnp.maximum(_layernorm(x, axis=-1), 0.0)
    x = x + _L0_gnn_ref(h, adj, L0_gnn_W1, L0_gnn_b1, L0_gnn_W2, L0_gnn_b2)
    h = jnp.maximum(_layernorm(x, axis=-1), 0.0)
    x = x + _L1_gnn_ref(h, adj, L1_gnn_W1, L1_gnn_b1, L1_gnn_g1, L1_gnn_be1, L1_gnn_W2, L1_gnn_b2, L1_gnn_g2, L1_gnn_be2)
    h = jnp.maximum(_layernorm(x, axis=-1), 0.0)
    x = x + _L2_gnn_ref(h, adj, L2_gnn_Wg0, L2_gnn_bg0, L2_gnn_Wg1, L2_gnn_bg1, L2_gnn_Wih, L2_gnn_Whh, L2_gnn_bih, L2_gnn_bhh)
    h = jnp.maximum(_layernorm(x, axis=-1), 0.0)
    x = x + _L3_gnn_ref(h, L3_gnn_W, adj)
    return x

_drawn_inputs = setup_inputs


def setup_inputs(seed=0):
    import zlib

    import numpy as np

    out = dict(_drawn_inputs(seed))
    spreads = {'L0_gnn_b1': (0.0, 0.1),
     'L0_gnn_b2': (0.0, 0.1),
     'L1_gnn_b1': (0.0, 0.8),
     'L1_gnn_g1': (1.0, 0.2),
     'L1_gnn_be1': (0.0, 0.1),
     'L1_gnn_b2': (0.0, 0.8),
     'L1_gnn_g2': (1.0, 0.2),
     'L1_gnn_be2': (0.0, 0.1),
     'L2_gnn_bg0': (0.0, 0.8),
     'L2_gnn_bg1': (0.0, 0.8)}
    factors = {'L2_gnn_Wg0': 8.0,
     'L2_gnn_Wg1': 8.0,
     'L2_gnn_Wih': 8.0,
     'L2_gnn_Whh': 8.0,
     'L2_gnn_bih': 4.547,
     'L2_gnn_bhh': 4.661}
    for name, (base, spread) in spreads.items():
        noise = np.random.default_rng([zlib.crc32(name.encode()), seed]).standard_normal(out[name].shape)
        drawn = base * np.exp(spread * noise) if base else spread * noise
        out[name] = jnp.asarray(drawn.astype(out[name].dtype))
    for name, factor in factors.items():
        out[name] = (out[name] * factor).astype(out[name].dtype)
    return out
```

```python
import numpy as np, concourse.bass as bass
from concourse import mybir
from contextlib import ExitStack
F=mybir.dt.float32; ALU=mybir.AluOpType; ACT=mybir.ActivationFunctionType; AX=mybir.AxisListType
N=128; K=N-2; W=64; LEAF=16; SWEEPS=16; PASSES=3
EPS=2.0**-24

class Chain:
    def __init__(self, eng, sem):
        self.eng, self.sem, self.n, self.dyn = eng, sem, 0, 0
    def mark(self, ins):
        ins.then_inc(self.sem, 1); self.n += 1
        return self.n + self.dyn
    def wait(self, value): self.eng.wait_ge(self.sem, value)
    def __call__(self, ins):
        self.wait(self.mark(ins))
    def loop(self, i, per): self.start, self.per, self.dyn = self.n, per, i*per
    def end(self, count):
        assert self.n-self.start==self.per,(self.n-self.start,self.per)
        self.n=self.start+self.per*count; self.dyn=0

def build(nc, ins, outs, NetCls=None):
  with ExitStack() as ctx:
    sb=lambda n,s,d=F: ctx.enter_context(nc.sbuf_tensor(n,s,d)); sem=lambda n: ctx.enter_context(nc.semaphore(n))
    adj=sb("adj",[N,N]); I=sb("I",[N,N]); MK=sb("MK",[N,N]); SUP=sb("SUP",[N,N]); ones=sb("ones",[N,N]); IOTA=sb("IOTA",[1,16]); IW=sb("IW",[N,W]); 
    iw32=sb("iw32",[N,W],mybir.dt.int32)
    adjT=sb("adjT",[N,N]); AhT=sb("AhT",[N,N]); dg=sb("dg",[N,32]); disD=sb("disD",[N,2*N]); disR=sb("disR",[N,2*N]); Ap=sb("Ap",[N,N]); tmp=sb("tmp",[N,N])
    B=sb("B",[N,N]); xc=sb("xc",[N,1]); bc=sb("bc",[N,1])
    R1=sb("R1",[N,16384]); V=R1[0:1,0:N*K]
    xr=sb("xr",[1,N]); br=sb("br",[1,N]); pr=sb("pr",[1,N]); wr=sb("wr",[1,N]); vt=sb("vt",[1,N]); jk=sb("jk",[1,N]); jk2=sb("jk2",[1,N]); sc=sb("sc",[1,32])
    Vr=sb("Vr",[N,N]); VrT=sb("VrT",[N,N]); M1=sb("M1",[N,N]); N1=sb("N1",[N,N]); M2=sb("M2",[N,N]); N2=sb("N2",[N,N]); Zm=sb("Zm",[N,N]); QT=sb("QT",[N,N])
    TD=sb("TD",[N,N]); TE=sb("TE",[N,N]); NE2=sb("NE2",[N,N]); tb=sb("tb",[N,2*N])
    w0=sb("w0",[1,16]); e2l=sb("e2l",[1,16]); dl=sb("dl",[1,16]); a16=sb("a16",[1,64]); st=sb("st",[1,16])
    lam=sb("lam",[N,W]); lo=sb("lob",[N,1]); hw=sb("hw",[N,1]); qa=sb("qa",[N,W]); ra=sb("ra",[N,W]); cnt=sb("cnt",[N,W]); cs=sb("cs",[N,8]); jcol=sb("jcol",[N,1]); jci=sb("jci",[N,1],mybir.dt.int32)
    l1=sb("l1",[N,8]); Dp=sb("Dp",[N,N]); Dm=sb("Dm",[N,N]); rp=sb("rp",[N,N]); rm=sb("rm",[N,N]); G=sb("G",[N,N]); mk=sb("mk",[N,N]); Y=sb("Y",[N,N]); Y2=sb("Y2",[N,N])
    u7=sb("u7",[N,8]); m7=sb("m7",[N,16]); sg=sb("sg",[N,16]); Yt=sb("Yt",[N,N]); X=sb("X",[N,N]); XT=sb("XT",[N,N]); U=sb("U",[N,N]); UT=sb("UT",[N,N]); Wm=sb("Wm",[N,N])
    P=[ctx.enter_context(nc.psum_tensor(f"P{i}",[128,512],F)) for i in range(8)]
    S={}
    def ev(n):
        if n not in S: S[n]=sem(n)
        return S[n]
    ctx.enter_context(nc.allow_non_contiguous_dma(reason="x")) if False else None
    NET=NetCls(nc,ins,sb,ev,P,(R1,U,UT,adjT,AhT,dg,I,ones,adj)) if NetCls else None
    block=ctx.enter_context(nc.Block())
    B3=R1[:,8192:16384].rearrange("p (i w) -> p i w",w=W)
    @block.sync
    def _(eng):
        eng.dma_start(adj[:,:],ins['adj']).then_inc(ev('adj_in'),16)
        if NET: NET.sync_load(eng)
        eng.wait_ge(ev('v_rows'),K); eng.wait_ge(ev('vr_zero'),1)
        eng.dma_start(Vr[0:K,:],V.rearrange("a (k n) -> a k n",n=N)).then_inc(ev('vr_in'),16)
        if NET:
            NET.sync_store(eng); return
        eng.wait_ge(ev('UT_ready'),1)
        for i,(o,t) in enumerate([('Bo',B),('TDo',TD),('TEo',TE),('Yo',Y),('QTo',QT),('Uo',U),('UTo',UT)]):
            eng.dma_start(outs[o],t[:,:]).then_inc(ev('out'),16)
        eng.dma_start(outs['lo'][:,0:7],l1[:,0:7]).then_inc(ev('out'),16)
        eng.dma_start(outs['sto'],st[:,:]).then_inc(ev('out'),16)
        eng.wait_ge(ev('out'),16*9)
    @block.gpsimd
    def _(eng):
        c=Chain(eng,ev('pool'))
        c.mark(eng.memset(I[:,:],0.0)); c.mark(eng.memset(MK[:,:],1.0)); c(eng.memset(SUP[:,:],0.0)) 
        eng.iota(iw32[:,:],pattern=[[1,W]],base=1,channel_multiplier=0).then_inc(ev('iota'),1)
        eng.iota(jci[:,:],pattern=[[1,1]],base=0,channel_multiplier=1).then_inc(ev('iota'),1)
        eng.affine_select(out=I[:,:],in_=I[:,:],compare_op=ALU.not_equal,fill=1.0,base=0,pattern=[[-1,N]],channel_multiplier=1).then_inc(ev('const'),1)
        eng.affine_select(out=MK[:,:],in_=MK[:,:],compare_op=ALU.is_gt,fill=0.0,base=0,pattern=[[-1,N]],channel_multiplier=1).then_inc(ev('const'),1)
        eng.affine_select(out=SUP[:,:],in_=SUP[:,:],compare_op=ALU.not_equal,fill=1.0,base=1,pattern=[[-1,N]],channel_multiplier=1).then_inc(ev('const'),1)
        eng.memset(Vr[:,:],0.0).then_inc(ev('vr_zero'),1)
        with eng.Fori(0,K) as k:
            eng.wait_ge(ev('v_done'),k+1)
            eng.tensor_copy(V[0:1,bass.ds(k*N,N)],xr[:,:]).then_inc(ev('v_rows'),1)
    @block.vector
    def _(v):
        c=Chain(v,ev('dve'))
        ts,tt,stt=v.tensor_scalar,v.tensor_tensor,v.scalar_tensor_tensor
        def ttr(o,a,b,acc,op0=ALU.mult,op1=ALU.add): return v.tensor_tensor_reduce(out=o,in0=a,in1=b,scale=1.0,scalar=0.0,op0=op0,op1=op1,accum_out=acc)
        v.memset(ones[:,:],1.0).then_inc(ev('ones'),1)
        v.wait_ge(ev('iota'),2)
        c(v.tensor_copy(IW[:,:],iw32[:,:])); c(v.tensor_copy(jcol[:,:],jci[:,:]))
        v.wait_ge(ev('adj_in'),16); v.wait_ge(ev('const'),3)
        c(ttr(tmp[:,:],adj[:,:],I[:,:],dg[:,0:1]))
        c(v.tensor_reduce(dg[:,1:2],adj[:,:],AX.X,ALU.add))
        c(tt(dg[:,2:3],dg[:,1:2],dg[:,0:1],ALU.subtract))
        v.wait_ge(ev('degT'),2)
        c(v.tensor_copy(adjT[:,:],P[0][:,0:N])); 
        c(tt(dg[:,3:4],dg[:,2:3],P[1][:,0:1],ALU.add))
        c(ts(dg[:,4:5],dg[:,3:4],1e-30,None,ALU.max)) ; c(ts(dg[:,5:6],dg[:,3:4],1.0,None,ALU.add)) 
        v.sem_inc(ev('deg'),1) if False else None
        c(ts(dg[:,16:17],dg[:,3:4],0.0,None,ALU.is_gt))
        v.wait_ge(ev('deg_sqrt'),1)
        c(v.reciprocal(dg[:,8:10],dg[:,6:8]))
        c(tt(dg[:,10:12],dg[:,4:6],dg[:,8:10],ALU.mult))
        c(tt(dg[:,10:12],dg[:,10:12],dg[:,6:8],ALU.add))
        c(ts(dg[:,10:12],dg[:,10:12],0.5,None,ALU.mult))
        c(v.reciprocal(dg[:,12:14],dg[:,10:12]))
        c(tt(dg[:,12:13],dg[:,12:13],dg[:,16:17],ALU.mult))
        c(ts(disD[:,0:N],I[:,:],dg[:,12:13],None,ALU.mult)); 
        ts(disD[:,N:2*N],I[:,:],dg[:,13:14],None,ALU.mult).then_inc(ev('disD'),1)
        c(tt(tmp[:,:],adj[:,:],adjT[:,:],ALU.add))
        c(ts(tmp[:,:],tmp[:,:],dg[:,12:13],-0.5,ALU.mult,ALU.mult))
        c(ts(dg[:,14:15],dg[:,3:4],dg[:,12:13],dg[:,12:13],ALU.mult,ALU.mult))
        c(ts(dg[:,15:16],dg[:,14:15],-1.0,None,ALU.add))
        v.wait_ge(ev('disR'),1)
        c(tt(tmp[:,:],tmp[:,:],P[2][:,0:N],ALU.mult))
        c(stt(Ap[:,:],I[:,:],dg[:,15:16],tmp[:,:],ALU.mult,ALU.add))
        c(v.tensor_copy(B[:,:],Ap[:,:]))
        c(tt(tmp[:,:],adjT[:,:],I[:,:],ALU.add))
        c(ts(tmp[:,:],tmp[:,:],dg[:,13:14],None,ALU.mult))
        c(tt(AhT[:,:],tmp[:,:],P[2][:,N:2*N],ALU.mult))
        with v.Fori(0,K) as k:
            ts(xc[:,:],B[:,bass.ds(k,1)],MK[:,bass.ds(k,1)],None,ALU.mult).then_inc(ev('xc'),1)
            v.wait_ge(ev('x'),k+1)
            v.tensor_copy(xr[:,:],P[0][0:1,0:N]).then_inc(ev('xr'),1)
            v.wait_ge(ev('xr'),k+1)
            c.loop(k,9)
            al=xr[0:1,bass.ds(k+1,1)]
            a=c.mark(ts(sc[:,0:1],al,0.0,2.0,ALU.is_ge,ALU.mult))
            v.wait_ge(ev('r'),k+1); c.wait(a)
            c.mark(ts(sc[:,1:2],sc[:,0:1],-1.0,sc[:,9:10],ALU.add,ALU.mult))
            c(stt(sc[:,2:3],sc[:,9:10],sc[:,9:10],sc[:,8:9],ALU.mult,ALU.add))
            a=c.mark(ts(sc[:,3:4],al,sc[:,1:2],None,ALU.mult))
            v.wait_ge(ev('br'),k+1); v.wait_ge(ev('y'),k+1)
            b=c.mark(stt(pr[:,:],br[:,:],sc[:,1:2],P[1][0:1,0:N],ALU.mult,ALU.add))
            c.wait(a)
            c.mark(ts(al,al,sc[:,1:2],None,ALU.add))
            c(stt(sc[:,4:5],sc[:,2:3],0.5,sc[:,3:4],ALU.mult,ALU.add))
            c.mark(ttr(jk[:,:],xr[:,:],pr[:,:],sc[:,5:6]))
            c(v.reciprocal(sc[:,10:11],sc[:,4:5]))
            v.wait_ge(ev('dve2'),2*k) if False else None
            ts(sc[:,6:7],sc[:,5:6],sc[:,10:11],-0.5,ALU.mult,ALU.mult).then_inc(ev('ng'),1)
            ts(vt[:,:],xr[:,:],sc[:,10:11],None,ALU.mult).then_inc(ev('v_done'),1)
            v.wait_ge(ev('ng'),k+1)
            stt(wr[:,:],xr[:,:],sc[:,6:7],pr[:,:],ALU.mult,ALU.add).then_inc(ev('w'),1)
            v.wait_ge(ev('o'),k+1)
            tt(B[:,:],B[:,:],P[3][:,0:N],ALU.subtract).then_inc(ev('B'),1)
            v.wait_ge(ev('B'),k+1)
            v.wait_ge(ev('v_rows'),k+1)
        c.end(K)
        c(tt(tb[:,0:N],B[:,:],I[:,:],ALU.mult)); tt(tb[:,N:2*N],B[:,:],SUP[:,:],ALU.mult).then_inc(ev('tb'),1)
        v.wait_ge(ev('trow'),1)
        c(v.tensor_copy(TD[:,:],P[2][:,0:N])); c(v.tensor_copy(TE[:,:],P[2][:,N:2*N]))
        c(stt(NE2[:,:],TE[:,:],-1.0,TE[:,:],ALU.mult,ALU.mult))
        c(ts(NE2[:,:],NE2[:,:],-1e-30,None,ALU.add))
        c(ts(dl[:,:],TD[0:1,0:16],1.0,None,ALU.add))
        c(stt(a16[:,0:1],TE[0:1,16:17],-1.0,TE[0:1,16:17],ALU.mult,ALU.max))
        c(tt(dl[:,15:16],dl[:,15:16],a16[:,0:1],ALU.subtract))
        c(ts(e2l[:,0:15],NE2[0:1,1:16],-1.0,None,ALU.mult))
        c(v.memset(st[:,:],1.0))
        with v.Fori(0,SWEEPS) as s_:
            RC=205
            c.loop(s_,RC-1)
            c(tt(a16[:,0:15],dl[:,0:15],dl[:,1:16],ALU.mult))
            c(stt(a16[:,0:15],a16[:,0:15],-1.0,a16[:,0:15],ALU.mult,ALU.max)); c(ts(a16[:,0:15],a16[:,0:15],EPS*EPS,None,ALU.mult))
            c(tt(a16[:,16:31],e2l[:,0:15],a16[:,0:15],ALU.is_gt))
            c(tt(e2l[:,0:15],e2l[:,0:15],a16[:,16:31],ALU.mult))
            c(tt(a16[:,0:15],IW[0:1,0:15],a16[:,16:31],ALU.mult))
            c(v.tensor_reduce(st[:,1:2],a16[:,0:15],AX.X,ALU.max))
            c(ts(a16[:,16:31],IW[0:1,0:15],st[:,1:2],None,ALU.is_equal))
            c(ttr(a16[:,0:15],a16[:,16:31],dl[:,1:16],st[:,2:3]))
            c(ttr(a16[:,0:15],a16[:,16:31],dl[:,0:15],st[:,3:4]))
            c(ttr(a16[:,0:15],a16[:,16:31],e2l[:,0:15],st[:,4:5]))
            c(ts(st[:,5:6],st[:,3:4],st[:,2:3],0.5,ALU.subtract,ALU.mult))
            stt(st[:,6:7],st[:,5:6],st[:,5:6],st[:,4:5],ALU.mult,ALU.add).then_inc(ev('rad2'),1)
            c(ts(st[:,7:8],st[:,5:6],0.0,2.0,ALU.is_ge,ALU.mult))
            v.wait_ge(ev('rad'),s_+1)
            c(ts(st[:,8:9],st[:,7:8],-1.0,st[:,9:10],ALU.add,ALU.mult))
            c(ts(st[:,8:9],st[:,8:9],st[:,5:6],1e-30,ALU.add,ALU.add))
            c(v.reciprocal(st[:,10:11],st[:,8:9]))
            c(ts(st[:,10:11],st[:,10:11],st[:,4:5],None,ALU.mult))
            c(tt(st[:,11:12],st[:,2:3],st[:,10:11],ALU.subtract))
            c(tt(st[:,12:13],dl[:,0:1],st[:,11:12],ALU.subtract))
            c(ts(st[:,7:8],st[:,12:13],0.0,-2.0,ALU.is_ge,ALU.mult))
            c(ts(st[:,13:14],st[:,1:2],0.5,None,ALU.is_ge))
            c(ts(st[:,7:8],st[:,7:8],st[:,13:14],1.0,ALU.mult,ALU.add))
            c(tt(st[:,0:1],st[:,0:1],st[:,7:8],ALU.mult))
            c(tt(st[:,13:14],st[:,12:13],st[:,12:13],ALU.mult))
            for i in range(15):
                s0=a16[:,40:41]; r=a16[:,41:42]; ri=a16[:,42:43]; cc=a16[:,43:44]; t=a16[:,44:45]; g2=a16[:,45:46]
                c(ts(r,e2l[:,i:i+1],st[:,13:14],1e-36,ALU.add,ALU.max))
                if i: c(ts(e2l[:,i-1:i],r,s0,None,ALU.mult))
                c(v.reciprocal(ri,r))
                c(ts(cc,ri,st[:,13:14],1e-30,ALU.mult,ALU.max))
                c(ts(s0,ri,e2l[:,i:i+1],None,ALU.mult))
                c(ts(t,s0,st[:,12:13],None,ALU.mult))
                c(ts(g2,dl[:,i+1:i+2],st[:,11:12],cc,ALU.subtract,ALU.mult))
                c(tt(g2,g2,t,ALU.subtract))
                c(ts(dl[:,i:i+1],dl[:,i+1:i+2],g2,st[:,12:13],ALU.subtract,ALU.add))
                c(v.reciprocal(ri,cc))
                c(ts(st[:,13:14],g2,g2,ri,ALU.mult,ALU.mult))
                c(v.tensor_copy(st[:,12:13],g2)) if False else None
                c(ts(st[:,12:13],g2,1.0,None,ALU.mult)) if i<14 else None
            c(ts(e2l[:,14:15],st[:,13:14],s0,None,ALU.mult))
            c(tt(dl[:,15:16],st[:,11:12],g2,ALU.add))
            c.per=c.n-c.start
            assert c.per==RC-1,(c.per,RC)
        c.end(SWEEPS)
        st_sign=c.n
        ab=tb
        c(stt(ab[:,0:N],TE[:,:],-1.0,TE[:,:],ALU.mult,ALU.max))
        c(tt(ab[:,N:2*N-1],ab[:,0:N-1],ab[:,1:N],ALU.add)); c(v.tensor_copy(ab[:,2*N-1:2*N],ab[:,N-1:N]))
        c(tt(ab[:,0:N],TD[:,:],ab[:,N:2*N],ALU.add)); c(v.tensor_reduce(cs[:,0:1],ab[:,0:N],AX.X,ALU.max))
        c(tt(ab[:,0:N],TD[:,:],ab[:,N:2*N],ALU.subtract)); c(v.tensor_reduce(cs[:,1:2],ab[:,0:N],AX.X,ALU.min))
        c(ts(cs[:,0:1],cs[:,0:1],1e-5,None,ALU.add)); c(ts(lo[:,:],cs[:,1:2],-1e-5,None,ALU.add))
        c(ts(hw[:,:],cs[:,0:1],lo[:,:],1.0/(W+1),ALU.subtract,ALU.mult))
        v.wait_ge(ev('vr_in'),16)
        with v.Fori(0,PASSES) as s_:
            PER=1+1+1+1+3*(N-1)+1+3
            b0=c.n
            c.loop(s_,PER)
            c(ts(lam[:,:],IW[:,:],hw[:,:],lo[:,:],ALU.mult,ALU.add))
            c(tt(B3, TD[:,:].unsqueeze(2).broadcast_to([N,N,W]), lam[:,:].unsqueeze(1).broadcast_to([N,N,W]), ALU.subtract))
            c(v.tensor_copy(qa[:,:],B3[:,0,:]))
            c.mark(ts(cnt[:,:],qa[:,:],0.0,None,ALU.is_lt))
            base=c.n
            with v.Fori(0,N-1) as i:
                c.dyn=s_*PER+i*3
                c.wait(c.n+c.dyn)
                c(v.reciprocal(ra[:,:],qa[:,:]))
                c(stt(qa[:,:],ra[:,:],NE2[:,bass.ds(i+1,1)],R1[:,bass.ds(8192+(i+1)*W,W)],ALU.mult,ALU.add))
                c.mark(stt(cnt[:,:],qa[:,:],0.0,cnt[:,:],ALU.is_lt,ALU.add))
            c.n=base+3*(N-1); c.dyn=s_*PER; c.wait(c.n+c.dyn)
            c(ts(qa[:,:],cnt[:,:],jcol[:,:],None,ALU.is_le))
            c(v.tensor_reduce(cs[:,2:3],qa[:,:],AX.X,ALU.add))
            c(stt(lo[:,:],cs[:,2:3],hw[:,:],lo[:,:],ALU.mult,ALU.add))
            c(ts(hw[:,:],hw[:,:],1.0/(W+1),None,ALU.mult))
        c.end(PASSES)
        c(ts(cs[:,3:4],hw[:,:],float(W+1),None,ALU.mult))
        c(stt(l1[:,0:1],cs[:,3:4],0.5,lo[:,:],ALU.mult,ALU.add)); c(tt(cs[:,4:5],lo[:,:],cs[:,3:4],ALU.add))
        NT=6+0
        with v.Fori(0,2) as s_:
            c.loop(s_,1)
            start=c.n
            PER=538
            c.dyn=s_*PER; c.per=PER
            c(ts(G[:,:],TD[:,:],l1[:,0:1],None,ALU.subtract))
            c.mark(v.tensor_copy(Dp[:,0:1],G[:,0:1])); f=c.mark(v.tensor_copy(Dm[:,N-1:N],G[:,N-1:N])); b=f
            for i in range(1,N):
                j=N-1-i
                c.wait(f); f=c.mark(v.reciprocal(rp[:,i-1:i],Dp[:,i-1:i]))
                c.wait(b); b=c.mark(v.reciprocal(rm[:,j+1:j+2],Dm[:,j+1:j+2]))
                c.wait(f); f=c.mark(ts(Dp[:,i:i+1],NE2[:,i:i+1],rp[:,i-1:i],G[:,i:i+1],ALU.mult,ALU.add))
                c.wait(b); b=c.mark(ts(Dm[:,j:j+1],NE2[:,j+1:j+2],rm[:,j+1:j+2],G[:,j:j+1],ALU.mult,ALU.add))
            c.wait(b)
            c(tt(G[:,:],G[:,:],Dp[:,:],ALU.subtract)); c(tt(G[:,:],Dm[:,:],G[:,:],ALU.subtract))
            c(tt(Y2[:,:],Dp[:,:],Dp[:,:],ALU.mult)); c(tt(Y[:,:],Dm[:,:],Dm[:,:],ALU.mult)); c(tt(Y2[:,:],Y2[:,:],Y[:,:],ALU.add)); c(tt(Y[:,:],G[:,:],G[:,:],ALU.mult)); c(stt(Y2[:,:],Y2[:,:],(8*EPS)**2,Y[:,:],ALU.mult,ALU.add)); c(v.tensor_reduce(cs[:,5:6],Y2[:,:],AX.X,ALU.min))
            c(ts(mk[:,:],Y2[:,:],cs[:,5:6],None,ALU.is_le))
            c(ttr(Y2[:,:],mk[:,:],G[:,:],cs[:,6:7]))
            c(ts(Y2[:,:],mk[:,:],1.0,None,ALU.subtract))
            c(tt(rm[:,1:N],rm[:,1:N],TE[:,1:N],ALU.mult)); c(tt(rm[:,1:N],rm[:,1:N],Y2[:,1:N],ALU.mult)); c(v.memset(rm[:,0:1],0.0))
            c(tt(rp[:,0:N-1],rp[:,0:N-1],TE[:,1:N],ALU.mult)); c(tt(rp[:,0:N-1],rp[:,0:N-1],Y2[:,0:N-1],ALU.mult)); c(v.memset(rp[:,N-1:N],0.0))
            c(v.tensor_tensor_scan(Y[:,:],rm[:,:],mk[:,:],0.0,ALU.mult,ALU.add))
            c(v.tensor_tensor_scan(Y2[:,::-1],rp[:,::-1],mk[:,::-1],0.0,ALU.mult,ALU.add))
            c(tt(Y[:,:],Y[:,:],Y2[:,:],ALU.add)); c(tt(Y[:,:],Y[:,:],mk[:,:],ALU.subtract))
            stt_=ttr(Y2[:,:],Y[:,:],Y[:,:],l1[:,2:3]); c(stt_)
            stt_=v.tensor_copy(l1[:,4:5],l1[:,2:3]); stt_.then_inc(ev('zz'),1)
            c(v.reciprocal(l1[:,3:4],l1[:,2:3]))
            c(ts(l1[:,5:6],cs[:,6:7],l1[:,3:4],l1[:,0:1],ALU.mult,ALU.add))
            c(ts(l1[:,0:1],l1[:,5:6],lo[:,:],cs[:,4:5],ALU.max,ALU.min))
            v.wait_ge(ev('zs'),s_+1)
            c(v.reciprocal(l1[:,6:7],l1[:,1:2]))
            c(ts(Y[:,:],Y[:,:],l1[:,6:7],None,ALU.mult))
            PERr=c.n-start
            assert PERr==PER
            c.per=PERr
        c.end(2)
        c(ts(m7[:,0:1],Y[:,0:1],0.0,2.0,ALU.is_ge,ALU.mult)); c(ts(m7[:,0:1],m7[:,0:1],-1.0,None,ALU.add))
        tt(st[:,14:15],st[:,0:1],st[:,0:1],ALU.mult).then_inc(ev('leaf'),1)
        v.wait_ge(ev('leafb'),1)
        c(ts(sg[:,0:1],m7[:,0:1],P[4][:,0:1],None,ALU.mult))
        c(tt(Y2[:,:],Y[:,:],Y[:,:],ALU.mult))
        c(v.tensor_reduce(m7[:,0:8],Y2[:,:].rearrange("p (a b) -> p a b",b=16),AX.X,ALU.add))
        c(ts(tb[:,0:N],I[:,:],l1[:,0:1],None,ALU.mult)); c(tt(tb[:,N:2*N],ones[:,:],tb[:,0:N],ALU.mult)) ; v.sem_inc(ev('lamd'),1)
        v.wait_ge(ev('lamr'),1)
        c(v.tensor_reduce(cs[:,0:1],P[5][:,0:N],AX.X,ALU.max)); c(ts(cs[:,0:1],cs[:,0:1],1.0,8*EPS,ALU.add,ALU.mult))
        def level(bs,h):
            for b in bs:
                c(ts(u7[:,0:1],TE[:,b:b+1],0.0,2.0,ALU.is_ge,ALU.mult)); c(ts(u7[:,0:1],u7[:,0:1],-1.0,Y[:,b:b+1],ALU.add,ALU.mult))
                c(tt(u7[:,0:1],u7[:,0:1],Y[:,b-1:b],ALU.add))
                c(tt(u7[:,1:2],u7[:,0:1],TE[:,b:b+1],ALU.mult)); c(stt(u7[:,1:2],u7[:,1:2],-1.0,u7[:,1:2],ALU.mult,ALU.max))
                c(ts(u7[:,1:2],u7[:,1:2],cs[:,0:1],None,ALU.is_gt))
                if h<64:
                    a0=(b-h)//16; a1=(b+h)//16
                    c(v.tensor_reduce(u7[:,2:3],m7[:,a0:a1],AX.X,ALU.add)); c(ts(u7[:,2:3],u7[:,2:3],0.5,None,ALU.is_gt)); c(tt(u7[:,1:2],u7[:,1:2],u7[:,2:3],ALU.mult))
                c(ts(u7[:,3:4],u7[:,0:1],0.0,-2.0,ALU.is_ge,ALU.mult)); c(ts(u7[:,3:4],u7[:,3:4],1.0,sg[:,0:1],ALU.add,ALU.subtract))
                c(stt(sg[:,0:1],u7[:,3:4],u7[:,1:2],sg[:,0:1],ALU.mult,ALU.add))
        level((16,48,80,112),16); level((32,96),32); level((64,),64)
        ts(Y[:,:],Y[:,:],sg[:,0:1],None,ALU.mult).then_inc(ev('Y'),1)
        c(ttr(tmp[:,:],Vr[:,:],Vr[:,:],dg[:,20:21])); c(ts(dg[:,20:21],dg[:,20:21],0.5,1e-30,ALU.mult,ALU.max)); v.sem_inc(ev('vv'),1)
        v.wait_ge(ev('vvs'),1)
        c(v.reciprocal(dg[:,22:23],dg[:,21:22])); ts(Vr[:,:],Vr[:,:],dg[:,22:23],None,ALU.mult).then_inc(ev('Vh'),1)
        v.wait_ge(ev('VhT'),1); v.tensor_copy(VrT[:,:],P[0][:,0:N]).then_inc(ev('VrT'),1)
        v.wait_ge(ev('gram'),1)
        c(tt(M1[:,:],P[1][:,0:N],MK[:,:],ALU.mult)) ; v.sem_inc(ev('M1'),1)
        v.wait_ge(ev('N1'),1); c(v.tensor_copy(N1[:,:],P[2][:,0:N]))
        c(tt(Zm[:,:],Vr[:,:],Vr[:,:],ALU.bypass)) if False else None
        v.sem_inc(ev('lev'),1)
        v.wait_ge(ev('nz'),1); c(tt(Zm[:,:],Vr[:,:],P[3][:,0:N],ALU.subtract))
        M=[M1,M2];Nn=[N1,N2]
        for s in range(6):
            a,b=s%2,(s+1)%2
            v.wait_ge(ev('sq'),s+1)
            c(v.tensor_copy(M[b][:,:],P[1][:,0:N])); c(v.tensor_copy(Nn[b][:,:],P[2][:,0:N])); v.sem_inc(ev('sqc'),1)
            v.wait_ge(ev('pz'),s+1)
            c(tt(Zm[:,:],Zm[:,:],P[3][:,0:N],ALU.add)); v.sem_inc(ev('zc'),1)
        v.wait_ge(ev('qq'),1)
        c(tt(QT[:,:],I[:,:],P[1][:,0:N],ALU.subtract)); c(v.tensor_copy(Yt[:,:],P[0][:,0:N])); v.sem_inc(ev('QT'),1)
        v.wait_ge(ev('X'),1); c(v.tensor_copy(X[:,:],P[2][:,0:N])); v.sem_inc(ev('Xs'),1)
        v.wait_ge(ev('WX'),1); c(v.tensor_copy(Wm[:,:],P[3][:,0:N])); c(v.tensor_copy(XT[:,:],P[0][:,0:N])); v.sem_inc(ev('Ws'),1)
        v.wait_ge(ev('SG'),1)
        Sx=P[1][:,0:N]; Gx=P[2][:,0:N]
        c(ttr(tmp[:,:],Sx,I[:,:],cs[:,0:1])); c(ttr(tmp[:,:],Gx,I[:,:],cs[:,1:2]))
        c(v.reciprocal(cs[:,2:3],cs[:,1:2])); c(ts(cs[:,3:4],cs[:,0:1],cs[:,2:3],None,ALU.mult))
        c(ts(tb[:,0:N],I[:,:],cs[:,3:4],None,ALU.mult)); v.sem_inc(ev('ld'),1)
        c(tt(tmp[:,:],I[:,:],Gx,ALU.subtract))
        v.wait_ge(ev('lr'),1)
        c(ts(Y2[:,:],P[3][:,0:N],cs[:,3:4],None,ALU.subtract))
        c(tt(G[:,:],P[3][:,0:N],tmp[:,:],ALU.mult)); c(tt(G[:,:],G[:,:],Sx,ALU.add))
        c(tt(mk[:,:],Y2[:,:],Y2[:,:],ALU.mult)); c(ts(mk[:,:],mk[:,:],4e-12,None,ALU.is_ge))
        c(ts(rp[:,:],mk[:,:],-1.0,-1.0,ALU.mult,ALU.subtract) if False else ts(rp[:,:],mk[:,:],-1.0,1.0,ALU.mult,ALU.add))
        c(tt(Y2[:,:],Y2[:,:],rp[:,:],ALU.add)); c(v.reciprocal(Y2[:,:],Y2[:,:]))
        c(tt(G[:,:],G[:,:],Y2[:,:],ALU.mult)); c(tt(G[:,:],G[:,:],mk[:,:],ALU.mult))
        c(tt(tmp[:,:],tmp[:,:],rp[:,:],ALU.mult)); c(stt(G[:,:],tmp[:,:],0.5,G[:,:],ALU.mult,ALU.add)); v.sem_inc(ev('E'),1)
        v.wait_ge(ev('XE'),1)
        c(tt(U[:,:],X[:,:],P[1][:,0:N],ALU.add)); c(tt(UT[:,:],XT[:,:],P[2][:,0:N],ALU.add)); v.sem_inc(ev('UT_ready'),1)
        if NET: NET.vec_pre(v,c); NET.vector(v,c)
    @block.scalar
    def _(a):
        a.preload_act_table(ACT.Sqrt)
        a.wait_ge(ev('dve'),9)
        a.activation(dg[:,6:8],dg[:,4:6],ACT.Sqrt).then_inc(ev('deg_sqrt'),1)
        with a.Fori(0,K) as k:
            a.wait_ge(ev('xc'),k+1)
            a.activation(bc[:,:],B[:,bass.ds(k+1,1)],ACT.Copy).then_inc(ev('bc'),1)
            a.wait_ge(ev('xr'),k+1)
            a.activation(jk2[:,:],xr[:,:],ACT.Square,accum_out=sc[:,8:9]).then_inc(ev('nn'),1)
            a.wait_ge(ev('nn'),k+1)
            a.activation(sc[:,9:10],sc[:,8:9],ACT.Sqrt).then_inc(ev('r'),1)
            a.wait_ge(ev('b'),k+1)
            a.activation(br[:,:],P[2][0:1,0:N],ACT.Copy).then_inc(ev('br'),1)
        with a.Fori(0,SWEEPS) as s_:
            a.wait_ge(ev('rad2'),s_+1)
            a.activation(st[:,9:10],st[:,6:7],ACT.Sqrt).then_inc(ev('rad'),1)
        if NET: NET.scalar_pre(a)
        with a.Fori(0,2) as s_:
            a.wait_ge(ev('zz'),s_+1)
            a.activation(l1[:,1:2],l1[:,4:5],ACT.Sqrt).then_inc(ev('zs'),1)
        a.wait_ge(ev('vv'),1)
        a.activation(dg[:,21:22],dg[:,20:21],ACT.Sqrt).then_inc(ev('vvs'),1)
        if NET: a.wait_ge(ev('UT_ready'),1); NET.scalar(a)
    @block.tensor
    def _(t):
        def mm(o,l,r,start=True,stop=True): return t.matmul(o,lhsT=l,rhs=r,start=start,stop=stop)
        t.wait_ge(ev('const'),3); t.wait_ge(ev('ones'),1); t.wait_ge(ev('adj_in'),16)
        t.transpose(P[0][:,0:N],adj[:,:],I[:,:]).then_inc(ev('degT'),1)
        mm(P[1][:,0:1],adj[:,:],ones[:,0:1]).then_inc(ev('degT'),1)
        t.wait_ge(ev('disD'),1)
        mm(P[2][:,0:2*N],ones[:,:],disD[:,:]).then_inc(ev('disR'),1)
        with t.Fori(0,K) as k:
            t.wait_ge(ev('xc'),k+1)
            mm(P[0][0:1,0:N],xc[:,:],I[:,:]).then_inc(ev('x'),1)
            mm(P[1][0:1,0:N],xc[:,:],B[:,:]).then_inc(ev('y'),1)
            t.wait_ge(ev('bc'),k+1)
            mm(P[2][0:1,0:N],bc[:,:],I[:,:]).then_inc(ev('b'),1)
            t.wait_ge(ev('w'),k+1)
            mm(P[3][:,0:N],vt[:,:],wr[:,:],stop=False)
            mm(P[3][:,0:N],wr[:,:],vt[:,:],start=False).then_inc(ev('o'),1)
        t.wait_ge(ev('tb'),1)
        mm(P[2][:,0:2*N],ones[:,:],tb[:,:]).then_inc(ev('trow'),1)
        if NET: NET.tensor_pre(t); t.wait_ge(ev('WT'),8)
        t.wait_ge(ev('leaf'),1)
        mm(P[4][:,0:1],ones[0:1,:],st[0:1,0:1]).then_inc(ev('leafb'),1)
        t.wait_ge(ev('lamd'),1)
        mm(P[5][:,0:N],ones[:,:],tb[:,0:N]).then_inc(ev('lamr'),1)
        t.wait_ge(ev('Vh'),1)
        t.transpose(P[0][:,0:N],Vr[:,:],I[:,:]).then_inc(ev('VhT'),1)
        t.wait_ge(ev('VrT'),1)
        mm(P[1][:,0:N],VrT[:,:],VrT[:,:]).then_inc(ev('gram'),1)
        t.wait_ge(ev('M1'),1)
        t.transpose(P[2][:,0:N],M1[:,:],I[:,:]).then_inc(ev('N1'),1)
        mm(P[3][:,0:N],M1[:,:],Vr[:,:]).then_inc(ev('nz'),1)
        t.wait_ge(ev('lev'),1)
        M=[M1,M2];Nn=[N1,N2]
        for s in range(6):
            a,b=s%2,(s+1)%2
            if s: t.wait_ge(ev('zc'),s)
            mm(P[1][:,0:N],Nn[a][:,:],M[a][:,:]); mm(P[2][:,0:N],M[a][:,:],Nn[a][:,:]).then_inc(ev('sq'),1)
            t.wait_ge(ev('sqc'),s+1)
            mm(P[3][:,0:N],M[b][:,:],Zm[:,:]).then_inc(ev('pz'),1)
        t.wait_ge(ev('zc'),6)
        t.wait_ge(ev('Y'),1)
        t.transpose(P[0][:,0:N],Y[:,:],I[:,:])
        mm(P[1][:,0:N],Zm[:,:],Vr[:,:]).then_inc(ev('qq'),1)
        t.wait_ge(ev('QT'),1)
        mm(P[2][:,0:N],QT[:,:],Yt[:,:]).then_inc(ev('X'),1)
        t.wait_ge(ev('Xs'),1)
        t.transpose(P[0][:,0:N],X[:,:],I[:,:])
        mm(P[3][:,0:N],Ap[:,:],X[:,:]).then_inc(ev('WX'),1)
        t.wait_ge(ev('Ws'),1)
        mm(P[1][:,0:N],X[:,:],Wm[:,:]); mm(P[2][:,0:N],X[:,:],X[:,:]).then_inc(ev('SG'),1)
        t.wait_ge(ev('ld'),1)
        mm(P[3][:,0:N],ones[:,:],tb[:,0:N]).then_inc(ev('lr'),1)
        t.wait_ge(ev('E'),1)
        mm(P[1][:,0:N],XT[:,:],G[:,:]); mm(P[2][:,0:N],G[:,:],XT[:,:]).then_inc(ev('XE'),1)
        if NET: t.wait_ge(ev('UT_ready'),1); NET.tensor(t)


BF=mybir.dt.bfloat16
NB=64; GB=4; C=GB*N; NG=NB//GB; NP=NG//2
class Net:
  def __init__(s, nc, A, sb, ev, P, T):
    s.A,s.ev,s.P=A,ev,P
    s.R1,s.U,s.UT,s.adjT,s.AhT,s.dg,s.I,s.ones,s.adj=T
    s.allocate(sb)
    s.rowof={}; q=0
    for n,k in (('L0_gnn_b1',1),('L1_gnn_b1',2),('L1_gnn_g1',2),('L1_gnn_be1',2),('L1_gnn_b2',1),('L1_gnn_g2',1),('L1_gnn_be2',1),('L2_gnn_bg1',1),('bih',16),('bhh',16)):
        s.rowof[n]=q; q+=k
  def allocate(s, sb):
    R1=s.R1
    slot=lambda i,n=C: R1[:,i*C:i*C+n]
    pair=lambda n: [sb(f"{n}{u}",[N,C]) for u in range(2)]
    s.xN=sb("xN",[N,NB*N]); s.R2=sb("R2",[N,NB*N])
    s.hb,s.zb,s.yb,s.ob,s.rb=(pair(n) for n in ("hb","zb","yb","ob","rb"))
    s.bst_all=sb("bst_all",[N,6*NB]); s.bst2=sb("bst2",[N,2*6*NG]); s.rsd=sb("rsd",[N,NB]); s.nmr=sb("nmr",[N,NB]); s.nt=sb("nt",[N,4*NB])
    s.bsc=sb("bsc",[N,4]); s.bsh=sb("bsh",[N,4]); s.bn=sb("bn",[N,16]); s.bnv=sb("bnv",[N,8]); s.mx=sb("mx",[N,16]); s.rc=sb("rc",[N,8])
    s.W0a=sb("W0a",[N,N]); s.W0b=sb("W0b",[N,N]); s.W1n=sb("W1n",[N,2,N]); s.W2n=sb("W2n",[N,2*N]); s.W1T=sb("W1T",[N,2,N]); s.W2T=sb("W2T",[N,2,N])
    s.Wg0=sb("Wg0",[N,N]); s.Wg1=sb("Wg1",[N,N]); s.Wqkv=sb("Wqkv",[N,3*N]); s.Wn=sb("Wn",[N,4,N]); s.WT=sb("WT",[N,32,N])
    s.NR=27; s.BR=sb("BR",[s.NR+16,N]); s.BC=sb("BC",[N,s.NR+16]); s.b2bc=sb("b2bc",[N,N]); s.bg0t=sb("bg0t",[N,N]); s.bg1t=sb("bg1t",[N,N]); s.bl=sb("bl",[N,16])
    s.mkb=sb("mkb",[N,N],BF); s.Ib=sb("Ib",[N,N],BF)
    s.cb=[slot(11+u) for u in range(2)]; s.gt=[[slot(13+4*u+k) for k in range(4)] for u in range(2)]; s.tcb=[slot(21+u) for u in range(2)]; s.hp=[slot(23+u) for u in range(2)]
    s.ee=[slot(h) for h in range(4)]; s.qb=slot(4); s.kb=slot(5); s.pT=[slot(6),slot(7)]; s.vx=[slot(8,GB*4*33).rearrange("p (b h d) -> p b h d",b=GB,h=4)]; s.at=slot(10,256)
  def sync_load(s, eng):
    A,ev=s.A,s.ev
    for q in range(4):
        eng.dma_start(s.xN[:,q*2048:(q+1)*2048].rearrange("n (b d) -> n b d",d=N), A['x'][q*16:(q+1)*16].rearrange("b n d -> n b d")).then_inc(ev(f'x_in'),16)
    for t,src in ((s.W0a[:,:],A['L0_gnn_W1']),(s.W0b[:,:],A['L0_gnn_W2']),(s.W1n[:,:,:],A['L1_gnn_W1'].rearrange("(g p) d -> p g d",p=N)),(s.W2n[:,:],A['L1_gnn_W2']),
                  (s.Wg0[:,:],A['L2_gnn_Wg0']),(s.Wg1[:,:],A['L2_gnn_Wg1']),(s.Wqkv[:,:],A['L3_gnn_W'])):
        eng.dma_start(t,src).then_inc(ev('w_in'),16)
    vec=lambda n: A[n].rearrange("(g n) -> g n",n=N)
    r=0
    s.row={}
    for n,k in (('L0_gnn_b1',1),('L1_gnn_b1',2),('L1_gnn_g1',2),('L1_gnn_be1',2),('L1_gnn_b2',1),('L1_gnn_g2',1),('L1_gnn_be2',1),('L2_gnn_bg1',1)):
        s.row[n]=r; eng.dma_start(s.BR[r:r+k,:],vec(n)).then_inc(ev('b_in'),16); r+=k
    s.row['bih']=r; eng.dma_start(s.BR[r:r+16,:],A['L2_gnn_bih'].rearrange("p (g n) -> (p g) n",n=N)).then_inc(ev('b_in'),16); r+=16
    s.row['bhh']=r; eng.dma_start(s.BR[r:r+16,:],A['L2_gnn_bhh'].rearrange("p (g n) -> (p g) n",n=N)).then_inc(ev('b_in'),16); r+=16
    assert r==s.NR+16, r
    eng.dma_start(s.b2bc[:,:],A['L0_gnn_b2'].rearrange("(a n) -> a n",a=1).broadcast_to([N,N])).then_inc(ev('b2_in'),16)
    eng.dma_start(s.bg0t[:,:],A['L2_gnn_bg0'].rearrange("(a n) -> a n",a=1).broadcast_to([N,N])).then_inc(ev('b2_in'),16)
    for q in range(8):
        if q: eng.wait_ge(ev('WnT'),q)
        eng.dma_start(s.Wn[:,:,:],A['L2_gnn_Wih' if q%2==0 else 'L2_gnn_Whh'][q//2].rearrange("(g p) d -> p g d",p=N)).then_inc(ev('Wn_in'),16)
  def sync_store(s, eng):
    ev=s.ev
    with eng.Fori(0,NG) as g:
        eng.wait_ge(ev('o_x'),g+1)
        eng.dma_start(s.A['out'][bass.ds(g*GB,GB)].rearrange("b n d -> n b d"), s.xN[:,bass.ds(g*C,C)].rearrange("n (b d) -> n b d",d=N)).then_inc(ev('out'),16)
    eng.wait_ge(ev('out'),16*NG)
  def ln_stats(s,v,x,g):
    for b in range(GB):
        v.bn_stats(s.bst_all[:,bass.ds(g*GB*6+b*6,6)], x[:,bass.ds(g*C+b*N,N)]).then_inc(s.ev('bst'),1)
  def rsqrt(s,v,c,var,tmp,out,k):
    c.mark(v.tensor_copy(tmp[0],var)); v.sem_inc(s.ev('sq_in'),1) if False else None
  def ln_final(s,v,c,k):
    ev=s.ev; bs=s.bst_all[:,:].rearrange("p (b s) -> p b s",s=6); nt=s.nt
    me,mo,M2e,M2o=bs[:,:,1],bs[:,:,4],bs[:,:,2],bs[:,:,5]
    a,b_,cc,d=(nt[:,i*NB:(i+1)*NB] for i in range(4))
    v.wait_ge(ev('bst'),k*NB)
    c(v.tensor_tensor(a,me,mo,ALU.add)); c(v.tensor_tensor(b_,me,mo,ALU.subtract)); c(v.tensor_tensor(cc,M2e,M2o,ALU.add))
    c(v.scalar_tensor_tensor(b_,b_,0.25,b_,ALU.mult,ALU.mult)); c(v.scalar_tensor_tensor(b_,cc,1.0/N,b_,ALU.mult,ALU.add))
    v.tensor_scalar(b_,b_,1e-5,None,ALU.add).then_inc(ev('ln_var'),1)
    v.wait_ge(ev('ln_sqrt'),k)
    c(v.reciprocal(d,cc)); c(v.tensor_tensor(d,d,b_,ALU.mult)); c(v.tensor_tensor(d,d,cc,ALU.add)); c(v.tensor_scalar(d,d,0.5,None,ALU.mult))
    c(v.reciprocal(s.rsd[:,:],d)); v.scalar_tensor_tensor(s.nmr[:,:],a,-0.5,s.rsd[:,:],ALU.mult,ALU.mult).then_inc(ev('ln'),1)
  def bn_final(s,v,c,k,stats,gamma,beta,nh,col):
    ev=s.ev; bn=s.bn; 
    for h in range(nh): c(v.bn_aggr(s.bnv[:,2*h:2*h+2],stats[:,h*6*NG:(h+1)*6*NG]))
    mean=s.bnv[:,0:2*nh:2]; var=s.bnv[:,1:2*nh:2]
    v.tensor_scalar(bn[:,0:nh],var,1e-5,None,ALU.add).then_inc(ev('bn_var'),1)
    v.wait_ge(ev('bn_sqrt'),k)
    c(v.reciprocal(bn[:,4:4+nh],bn[:,2:2+nh])); c(v.tensor_tensor(bn[:,4:4+nh],bn[:,4:4+nh],bn[:,0:nh],ALU.mult)); c(v.tensor_tensor(bn[:,4:4+nh],bn[:,4:4+nh],bn[:,2:2+nh],ALU.add)); c(v.tensor_scalar(bn[:,4:4+nh],bn[:,4:4+nh],0.5,None,ALU.mult))
    c(v.reciprocal(bn[:,6:6+nh],bn[:,4:4+nh]))
    c(v.tensor_tensor(s.bsc[:,col:col+nh],bn[:,6:6+nh],gamma,ALU.mult))
    c(v.tensor_tensor(bn[:,8:8+nh],mean,s.bsc[:,col:col+nh],ALU.mult))
    v.tensor_tensor(s.bsh[:,col:col+nh],beta,bn[:,8:8+nh],ALU.subtract).then_inc(ev('bn'),1)
  def vec_pre(s,v,c):
    ev=s.ev
    v.tensor_copy(s.Ib[:,:],s.I[:,:]).then_inc(ev('mask'),1); v.tensor_scalar(s.mkb[:,:],s.adj[:,:],0.0,-1e30,ALU.is_equal,ALU.mult).then_inc(ev('mask'),1)
    v.wait_ge(ev('x_in'),64)
    with v.Fori(0,NG) as g: s.ln_stats(v,s.xN,g)
  def bcol(s,n,k=1): r=s.rowof[n]; return s.BC[:,r:r+k]
  def vector(s,v,c):
    ev=s.ev; tt,ts,stt=v.tensor_tensor,v.tensor_scalar,v.scalar_tensor_tensor; P=s.P; xN=s.xN; R1,R2=s.R1,s.R2
    X=lambda g: xN[:,bass.ds(g*C,C)]
    b4=lambda t: t[:,:].unsqueeze(1).broadcast_to([N,GB,N])
    g4=lambda t: t.rearrange("p (b d) -> p b d",d=N)
    v.wait_ge(ev('BCp'),1); v.wait_ge(ev('rsrow'),1); c(v.tensor_copy(s.BC[:,:],P[6][:,N:N+s.NR+16]))
    c(tt(s.bl[:,:],s.bcol('bih',16),s.bcol('bhh',16),ALU.add))
    v.wait_ge(ev('b2_in'),32); v.wait_ge(ev('rsrow'),1)
    c(ts(s.bg0t[:,:],s.bg0t[:,:],s.dg[:,1:2],None,ALU.mult)); ts(s.bg1t[:,:],P[6][:,0:N],s.bcol('L2_gnn_bg1'),None,ALU.mult).then_inc(ev('biases'),1)
    v.wait_ge(ev('biases'),1)
    s.ln_final(v,c,1)
    v.sem_inc(ev('a_x'),2)
    with v.Fori(0,NP) as it:
        for u in range(2):
            v.wait_ge(ev('a_mA'),2*it+u+1); v.tensor_copy(s.zb[u][:,:],P[u][:,:]).then_inc(ev('a_z'),1)
        for u in range(2):
            v.wait_ge(ev('a_mC'),2*it+u+1); tt(g4(s.ob[u][:,:]),g4(P[4+u][:,:]),b4(s.b2bc),ALU.add).then_inc(ev('a_o'),1)
        for u in range(2):
            g=2*it+u
            v.wait_ge(ev('a_mD'),2*it+u+1); tt(X(g),X(g),P[6+u][:,:],ALU.add).then_inc(ev('a_x'),1)
            v.wait_ge(ev('a_x'),2*it+u+3)
            s.ln_stats(v,xN,g)
    s.ln_final(v,c,2)
    v.sem_inc(ev('b_h'),2)
    with v.Fori(0,NP) as it:
        for u in range(2):
            v.wait_ge(ev('b_mA'),2*it+u+1); v.tensor_copy(s.zb[u][:,:],P[u][:,:]).then_inc(ev('b_z'),1)
        for u in range(2):
            g=2*it+u; Hb=R1[:,bass.ds(8192+g*C,C)]
            v.wait_ge(ev('b_mB'),2*it+u+1); ts(Hb,P[4+u][:,:],s.bcol('L1_gnn_b1',2)[:,1:2],None,ALU.add).then_inc(ev('b_h'),1)
            v.wait_ge(ev('b_h'),2*it+u+3); v.bn_stats(s.bst2[:,bass.ds(6*NG+g*6,6)],Hb).then_inc(ev('bst2'),1)
            v.wait_ge(ev('b_ha'),2*it+u+3)
            v.bn_stats(s.bst2[:,bass.ds(g*6,6)],R1[:,bass.ds(g*C,C)]).then_inc(ev('bst2'),1)
    v.wait_ge(ev('bst2'),2*NG)
    s.bn_final(v,c,1,s.bst2,s.bcol('L1_gnn_g1',2),s.bcol('L1_gnn_be1',2),2,0)
    v.sem_inc(ev('c_o'),2)
    with v.Fori(0,NP) as it:
        for u in range(2):
            g=2*it+u
            v.wait_ge(ev('c_m'),2*it+u+3); ts(R2[:,bass.ds(g*C,C)],P[u][:,:],s.bcol('L1_gnn_b2'),None,ALU.add).then_inc(ev('c_o'),1)
            v.wait_ge(ev('c_o'),2*it+u+3); v.bn_stats(s.bst2[:,bass.ds(g*6,6)],R2[:,bass.ds(g*C,C)]).then_inc(ev('bst2'),1)
    v.wait_ge(ev('bst2'),3*NG)
    s.bn_final(v,c,2,s.bst2,s.bcol('L1_gnn_g2'),s.bcol('L1_gnn_be2'),1,2)
    v.sem_inc(ev('d_x'),2)
    with v.Fori(0,NP) as it:
        for u in range(2):
            g=2*it+u
            v.wait_ge(ev('d_m'),2*it+u+3); tt(X(g),X(g),P[u][:,:],ALU.add).then_inc(ev('d_x'),1)
            v.wait_ge(ev('d_x'),2*it+u+3); s.ln_stats(v,xN,g)
    s.ln_final(v,c,3)
    v.sem_inc(ev('e_o'),2)
    with v.Fori(0,NP) as it:
        for u in range(2):
            v.wait_ge(ev('e_mA'),2*it+u+1); v.tensor_copy(s.zb[u][:,:],P[u][:,:]).then_inc(ev('e_z'),1)
        for u in range(2):
            v.wait_ge(ev('e_mB'),2*it+u+1); tt(g4(s.yb[u][:,:]),g4(P[2+u][:,:]),b4(s.bg0t),ALU.add).then_inc(ev('e_y'),1)
        for u in range(2):
            v.wait_ge(ev('e_mD'),2*it+u+1); tt(g4(s.cb[u][:,:]),g4(P[6+u][:,:]),b4(s.bg1t),ALU.add).then_inc(ev('e_o'),1)
    v.sem_inc(ev('l_h'),2)
    base=0
    for p in range(1,5):
        BG,nw,cols,NGp=s.lstm_shape(p)
        with v.Fori(0,NGp//2) as it:
            for st in range(p):
                for u in range(2):
                    k=base+2*(it*p+st)+u+1
                    gi,gf,gg,go=(t[:,0:cols] for t in s.gt[u]); cbu=s.cb[u][:,0:cols]
                    v.wait_ge(ev('l_g'),k+2)
                    if st==0: tt(cbu,gi,gg,ALU.mult).then_inc(ev('l_c'),1)
                    else:
                        tt(gi,gi,gg,ALU.mult).then_inc(ev('l_ig'),1)
                        tt(cbu,cbu,gf,ALU.mult).then_inc(ev('l_ig'),1)
                        v.wait_ge(ev('l_ig'),s.igb[p]+4*(it*(p-1)+st-1)+2*u+2)
                        tt(cbu,cbu,gi,ALU.add).then_inc(ev('l_c'),1)
                for u in range(2):
                    k=base+2*(it*p+st)+u+1
                    go=s.gt[u][3][:,0:cols]; tc=s.tcb[u][:,0:cols]
                    v.wait_ge(ev('l_t'),k)
                    if st<p-1: tt(s.hp[u][:,0:cols],go,tc,ALU.mult).then_inc(ev('l_h'),1)
                    else: tt(s.win(2*it+u,p,st),go.rearrange("p (b w) -> p b w",w=nw),tc.rearrange("p (b w) -> p b w",w=nw),ALU.mult).then_inc(ev('l_h'),1)
        base+=NGp*p
    v.sem_inc(ev('f_x'),2)
    with v.Fori(0,NP) as it:
        for u in range(2):
            g=2*it+u
            v.wait_ge(ev('f_m'),2*it+u+3); tt(X(g),X(g),P[u][:,:],ALU.add).then_inc(ev('f_x'),1)
            v.wait_ge(ev('f_x'),2*it+u+3); s.ln_stats(v,xN,g)
    s.ln_final(v,c,4)
    v.memset(s.vx[0][:,:,:,:],1.0).then_inc(ev('vx1'),1)
    v.wait_ge(ev('vx1'),1); v.sem_inc(ev('o_xh'),1)
    with v.Fori(0,NG) as g:
        v.wait_ge(ev('o_hT'),g+1); v.tensor_copy(s.zb[0][:,:],P[0][:,:]).then_inc(ev('o_z'),1)
        v.wait_ge(ev('o_k'),g+1); v.tensor_copy(s.kb[:,:],P[2][:,:]).then_inc(ev('o_kb'),1)
        v.wait_ge(ev('o_v'),g+1); v.tensor_copy(s.vx[0][:,:,:,0:32],P[0][:,:].rearrange("p (b h d) -> p b h d",b=GB,h=4)).then_inc(ev('o_vb'),1)
        for h in range(4):
            v.wait_ge(ev('o_s'),4*g+h+1)
            S3=g4(P[4+h][:,:])
            v.tensor_reduce(s.mx[:,h*4:h*4+4],S3,AX.X,ALU.max).then_inc(ev('o_mx'),1)
            v.wait_ge(ev('o_mx'),4*g+h+1)
            tt(g4(s.ee[h][:,:]),S3,s.mx[:,h*4:h*4+4].unsqueeze(2).broadcast_to([N,GB,N]),ALU.subtract).then_inc(ev('o_sub'),1)
        for h in range(4):
            v.wait_ge(ev('o_pt'),4*g+h+1)
            v.tensor_copy(s.pT[h%2][:,:],P[1+h%2][:,:]).then_inc(ev('o_ptc'),1)
        for hh in range(2):
            v.wait_ge(ev('o_pv'),2*g+hh+1)
            O=P[3 if hh==0 else 0][:,0:2*GB*33].rearrange("p (h b d) -> p h b d",h=2,b=GB)
            v.reciprocal(s.rc[:,:],O[:,:,:,32].rearrange("p h b -> p h b") if False else P[3 if hh==0 else 0][:,32:2*GB*33:33]).then_inc(ev('o_rc'),1)
            v.wait_ge(ev('o_rc'),2*g+hh+1)
            tmp=s.at[:,:].rearrange("p (h b d) -> p h b d",h=2,b=GB)
            tt(tmp,O[:,:,:,0:32],s.rc[:,:].rearrange("p (h b) -> p h b",h=2).unsqueeze(3).broadcast_to([N,2,GB,32]),ALU.mult).then_inc(ev('o_at'),1)
            v.wait_ge(ev('o_at'),2*g+hh+1)
            xs=X(g).rearrange("p (b h d) -> p h b d",b=GB,h=4)[:,2*hh:2*hh+2]
            i_=tt(xs,xs,tmp,ALU.add)
            i_.then_inc(ev('o_xh'),1)
        v.wait_ge(ev('o_xh'),2*g+3); v.sem_inc(ev('o_x'),1)
  def lstm_shape(s,p):
    BG={1:4,2:8,3:8,4:16}[p]; nw=N//p
    return BG,nw,BG*nw,NB//BG
  igb={1:0,2:0,3:2*8*1,4:2*8*1+2*8*2}
  def win(s,g,p,st):
    BG,nw,cols,_=s.lstm_shape(p)
    return s.R2[:,bass.ds(g*BG*N,BG*N)].rearrange("p (b t) -> p b t",t=N)[:,:,st:st+(nw-1)*p+1:p]
  def act_ln(s,a,it,pfx):
    for u in range(2):
        for b in range(GB):
            col=(2*it+u)*GB+b
            i=a.activation(s.hb[u][:,b*N:(b+1)*N],s.xN[:,bass.ds((2*it+u)*C+b*N,N)],ACT.Relu,bias=s.nmr[:,bass.ds(col,1)],scale=s.rsd[:,bass.ds(col,1)])
            if b==GB-1: i.then_inc(s.ev(pfx+'hl'),1)
  def act_ln_sqrt(s,a,k):
    a.wait_ge(s.ev('ln_var'),k); a.activation(s.nt[:,2*NB:3*NB],s.nt[:,NB:2*NB],ACT.Sqrt).then_inc(s.ev('ln_sqrt'),1); a.wait_ge(s.ev('ln'),k)
  def scalar(s,a):
    ev=s.ev; P=s.P; R1,R2=s.R1,s.R2; act=a.activation
    a.preload_act_table(ACT.Sqrt)
    s.act_ln_sqrt(a,1); a.wait_ge(ev('biases'),1)
    s.scalar_main(a)
  def scalar_pre(s,a):
    ev=s.ev; P=s.P; act=a.activation
    for q in range(2):
        a.wait_ge(ev('W12T'),q+1); act((s.W1T if q==0 else s.W2T)[:,:,:].rearrange("p g n -> p (g n)"),P[7][:,q*256:q*256+256],ACT.Copy).then_inc(ev('W12'),1)
    for q in range(8):
        a.wait_ge(ev('WnT'),q+1); act(s.WT[:,4*q:4*q+4,:].rearrange("p g n -> p (g n)"),P[4][:,:],ACT.Copy).then_inc(ev('WT'),1)
  def scalar_main(s,a):
    ev=s.ev; P=s.P; R1,R2=s.R1,s.R2; act=a.activation
    with a.Fori(0,NP) as it:
        s.act_ln(a,it,'a_')
        for u in range(2):
            a.wait_ge(ev('a_mB'),2*it+u+1); act(s.rb[u][:,:],P[2+u][:,:],ACT.Relu,bias=s.bcol('L0_gnn_b1')).then_inc(ev('a_r'),1)
    s.act_ln_sqrt(a,2)
    a.sem_inc(ev('b_ha'),2)
    with a.Fori(0,NP) as it:
        s.act_ln(a,it,'b_')
        for u in range(2):
            g=2*it+u
            a.wait_ge(ev('b_mB'),2*it+u+1); act(R1[:,bass.ds(g*C,C)],P[2+u][:,:],ACT.Identity,bias=s.bcol('L1_gnn_b1',2)[:,0:1]).then_inc(ev('b_ha'),1)
    a.wait_ge(ev('bn_var'),1); act(s.bn[:,2:4],s.bn[:,0:2],ACT.Sqrt).then_inc(ev('bn_sqrt'),1); a.wait_ge(ev('bn'),1)
    a.sem_inc(ev('dummy'),2) if False else None
    with a.Fori(0,NP) as it:
        for u in range(2):
            g=2*it+u
            a.wait_ge(ev('c_m'),2*it+u+1)
            act(s.hb[u][:,:],R1[:,bass.ds(g*C,C)],ACT.Relu,bias=s.bsh[:,0:1],scale=s.bsc[:,0:1])
            act(s.yb[u][:,:],R1[:,bass.ds(8192+g*C,C)],ACT.Relu,bias=s.bsh[:,1:2],scale=s.bsc[:,1:2]).then_inc(ev('c_h'),1)
    a.wait_ge(ev('bn_var'),2); act(s.bn[:,2:3],s.bn[:,0:1],ACT.Sqrt).then_inc(ev('bn_sqrt'),1); a.wait_ge(ev('bn'),2)
    with a.Fori(0,NP) as it:
        for u in range(2):
            g=2*it+u
            a.wait_ge(ev('d_m'),2*it+u+1)
            act(s.zb[u][:,:],R2[:,bass.ds(g*C,C)],ACT.Identity,bias=s.bsh[:,2:3],scale=s.bsc[:,2:3]).then_inc(ev('d_z'),1)
    s.act_ln_sqrt(a,3)
    with a.Fori(0,NP) as it:
        s.act_ln(a,it,'e_')
        for u in range(2):
            a.wait_ge(ev('e_y'),2*it+u+1); act(s.rb[u][:,:],s.yb[u][:,:],ACT.Relu).then_inc(ev('e_r'),1)
        for u in range(2):
            a.wait_ge(ev('e_mC'),2*it+u+1); act(s.ob[u][:,:],P[4+u][:,:],ACT.Copy).then_inc(ev('e_c'),1)
        for u in range(2):
            g=2*it+u
            a.wait_ge(ev('e_o'),2*it+u+3); act(R2[:,bass.ds(g*C,C)],s.cb[u][:,:],ACT.Relu).then_inc(ev('e_g'),1)
    a.preload_act_table(ACT.Sigmoid)
    a.sem_inc(ev('l_g'),2)
    base=0
    for p in range(1,5):
        BG,nw,cols,NGp=s.lstm_shape(p)
        with a.Fori(0,NGp//2) as it:
            for st in range(p):
                for u in range(2):
                    k=base+2*(it*p+st)+u+1
                    a.wait_ge(ev('l_m'),k); a.wait_ge(ev('l_h'),k)
                    for gate,f in ((0,ACT.Sigmoid),(2,ACT.Tanh))+(((1,ACT.Sigmoid),) if st else ())+((3,ACT.Sigmoid),):
                        i=act(s.gt[u][gate][:,0:cols],P[4*u+gate][:,0:cols],f,bias=s.bl[:,4*(p-1)+gate:4*(p-1)+gate+1])
                    i.then_inc(ev('l_g'),1)
                for u in range(2):
                    k=base+2*(it*p+st)+u+1
                    a.wait_ge(ev('l_c'),k); act(s.tcb[u][:,0:cols],s.cb[u][:,0:cols],ACT.Tanh).then_inc(ev('l_t'),1)
        base+=NGp*p
    a.preload_act_table(ACT.Sqrt)
    a.wait_ge(ev('l_h'),base+2)
    with a.Fori(0,NP) as it:
        for u in range(2):
            a.wait_ge(ev('f_m'),2*it+u+1)
            act(s.zb[u][:,:],R2[:,bass.ds((2*it+u)*C,C)],ACT.Copy).then_inc(ev('f_z'),1)
    s.act_ln_sqrt(a,4)
    a.preload_act_table(ACT.Exp)
    with a.Fori(0,NG) as g:
        for b in range(GB):
            i=act(s.hb[0][:,b*N:(b+1)*N],s.xN[:,bass.ds(g*C+b*N,N)],ACT.Relu,bias=s.nmr[:,bass.ds(g*GB+b,1)],scale=s.rsd[:,bass.ds(g*GB+b,1)])
        i.then_inc(ev('o_h'),1)
        a.wait_ge(ev('o_q'),g+1); act(s.qb[:,:],P[1][:,:],ACT.Copy,scale=float(32**-0.5)).then_inc(ev('o_qb'),1)
        for h in range(4):
            a.wait_ge(ev('o_sub'),4*g+h+1); act(s.ee[h][:,:],s.ee[h][:,:],ACT.Exp).then_inc(ev('o_e'),1)
  def tensor_pre(s,t):
    ev=s.ev; P=s.P; I=s.I[:,:]
    t.wait_ge(ev('w_in'),16*7)
    for g in range(2): i=t.transpose(P[7][:,g*N:(g+1)*N],s.W1n[:,g,:],I)
    i.then_inc(ev('W12T'),1)
    t.wait_ge(ev('W12'),1)
    for g in range(2): i=t.transpose(P[7][:,(2+g)*N:(3+g)*N],s.W2n[:,g*N:(g+1)*N],I)
    i.then_inc(ev('W12T'),1)
    for q in range(8):
        t.wait_ge(ev('Wn_in'),16*(q+1))
        if q: t.wait_ge(ev('WT'),q)
        for g in range(4): i=t.transpose(P[4][:,g*N:(g+1)*N],s.Wn[:,g,:],I)
        i.then_inc(ev('WnT'),1)
        if q<7: i=t.sem_inc(ev('Wn_free'),1) if False else None
    t.wait_ge(ev('b_in'),160)
    nr=s.NR+16
    t.transpose(P[6][:,N:N+nr],s.BR[:,:],s.I[0:nr,0:nr]).then_inc(ev('BCp'),1)
    t.matmul(P[6][:,0:N],lhsT=s.ones[:,:],rhs=s.adjT[:,:],start=True,stop=True).then_inc(ev('rsrow'),1)
  def tensor(s,t):
    ev=s.ev; P=s.P; I=s.I
    def mm(o,l,r,start=True,stop=True,**k): return t.matmul(o,lhsT=l,rhs=r,start=start,stop=stop,**k)
    def mix(dst,src,M):
        for b in range(GB): i=mm(dst[:,b*N:(b+1)*N],src[:,b*N:(b+1)*N],M)
        return i
    t.wait_ge(ev('W12'),2); t.wait_ge(ev('WT'),8)
    with t.Fori(0,NP) as it:
        for u in range(2): t.wait_ge(ev('a_hl'),2*it+u+1); mix(P[u],s.hb[u],s.U[:,:]).then_inc(ev('a_mA'),1)
        for u in range(2): t.wait_ge(ev('a_z'),2*it+u+1); mm(P[2+u][:,:],s.W0a[:,:],s.zb[u][:,:]).then_inc(ev('a_mB'),1)
        for u in range(2): t.wait_ge(ev('a_r'),2*it+u+1); mix(P[4+u],s.rb[u],s.W0b[:,:]).then_inc(ev('a_mC'),1)
        for u in range(2): t.wait_ge(ev('a_o'),2*it+u+1); t.wait_ge(ev('a_x'),2*it+u+1); mm(P[6+u][:,:],s.UT[:,:],s.ob[u][:,:]).then_inc(ev('a_mD'),1)
    with t.Fori(0,NP) as it:
        for u in range(2): t.wait_ge(ev('b_hl'),2*it+u+1); mix(P[u],s.hb[u],s.AhT[:,:]).then_inc(ev('b_mA'),1)
        for u in range(2):
            t.wait_ge(ev('b_z'),2*it+u+1); t.wait_ge(ev('b_h'),2*it+u+1); t.wait_ge(ev('b_ha'),2*it+u+1)
            mm(P[2+u][:,:],s.W1T[:,0,:],s.zb[u][:,:]); mm(P[4+u][:,:],s.W1T[:,1,:],s.zb[u][:,:]).then_inc(ev('b_mB'),1)
    t.sem_inc(ev('c_m'),2)
    with t.Fori(0,NP) as it:
        for u in range(2):
            t.wait_ge(ev('c_h'),2*it+u+1); t.wait_ge(ev('c_o'),2*it+u+1)
            mm(P[u][:,:],s.W2T[:,0,:],s.hb[u][:,:],stop=False); mm(P[u][:,:],s.W2T[:,1,:],s.yb[u][:,:],start=False).then_inc(ev('c_m'),1)
    t.sem_inc(ev('d_m'),2)
    with t.Fori(0,NP) as it:
        for u in range(2):
            t.wait_ge(ev('d_z'),2*it+u+1); t.wait_ge(ev('d_x'),2*it+u+1)
            for b in range(GB): i=t.transpose(P[u][:,b*N:(b+1)*N],s.zb[u][:,b*N:(b+1)*N],I[:,:])
            i.then_inc(ev('d_m'),1)
    with t.Fori(0,NP) as it:
        for u in range(2): t.wait_ge(ev('e_hl'),2*it+u+1); mix(P[u],s.hb[u],s.adjT[:,:]).then_inc(ev('e_mA'),1)
        for u in range(2): t.wait_ge(ev('e_z'),2*it+u+1); mix(P[2+u],s.zb[u],s.Wg0[:,:]).then_inc(ev('e_mB'),1)
        for u in range(2): t.wait_ge(ev('e_r'),2*it+u+1); mix(P[4+u],s.rb[u],s.adjT[:,:]).then_inc(ev('e_mC'),1)
        for u in range(2): t.wait_ge(ev('e_c'),2*it+u+1); t.wait_ge(ev('e_o'),2*it+u+1); mm(P[6+u][:,:],s.Wg1[:,:],s.ob[u][:,:]).then_inc(ev('e_mD'),1)
    t.wait_ge(ev('e_g'),NG); t.wait_ge(ev('e_o'),NG+2)
    base=0
    for p in range(1,5):
        BG,nw,cols,NGp=s.lstm_shape(p)
        if base: t.wait_ge(ev('l_h'),base+2)
        with t.Fori(0,NGp//2) as it:
            for st in range(p):
                for u in range(2):
                    k=base+2*(it*p+st)+u+1
                    gates=(0,2,1,3) if st else (0,2,3)
                    t.wait_ge(ev('l_g'),k)
                    xs=s.win(2*it+u,p,st)
                    for gate in gates: i=mm(P[4*u+gate][:,0:cols].rearrange("p (b w) -> p b w",w=nw),s.WT[:,(2*(p-1))*4+gate,:],xs,stop=(st==0))
                    if st:
                        t.wait_ge(ev('l_h'),k)
                        for gate in gates: i=mm(P[4*u+gate][:,0:cols],s.WT[:,(2*(p-1)+1)*4+gate,:],s.hp[u][:,0:cols],start=False)
                    i.then_inc(ev('l_m'),1)
        base+=NGp*p
    t.wait_ge(ev('l_h'),base+2)
    t.sem_inc(ev('f_m'),2)
    with t.Fori(0,NP) as it:
        for u in range(2):
            g=2*it+u
            t.wait_ge(ev('f_z'),2*it+u+1); t.wait_ge(ev('f_x'),2*it+u+1)
            for b in range(GB): i=t.transpose(P[u][:,b*N:(b+1)*N],s.zb[u][:,b*N:(b+1)*N],I[:,:])
            i.then_inc(ev('f_m'),1)
    t.wait_ge(ev('mask'),2)
    t.wait_ge(ev('f_x'),NG+2)
    with t.Fori(0,NG) as g:
        t.wait_ge(ev('o_h'),g+1); t.wait_ge(ev('o_xh'),2*g+1)
        for b in range(GB): i=t.transpose(P[0][:,b*N:(b+1)*N],s.hb[0][:,b*N:(b+1)*N],I[:,:])
        i.then_inc(ev('o_hT'),1)
        t.wait_ge(ev('o_z'),g+1)
        mm(P[1][:,:],s.Wqkv[:,0:N],s.zb[0][:,:]).then_inc(ev('o_q'),1)
        mm(P[2][:,:],s.Wqkv[:,N:2*N],s.zb[0][:,:]).then_inc(ev('o_k'),1)
        mix(P[0],s.zb[0],s.Wqkv[:,2*N:3*N]).then_inc(ev('o_v'),1)
        t.wait_ge(ev('o_qb'),g+1); t.wait_ge(ev('o_kb'),g+1)
        for h in range(4):
            r=slice(32*h,32*h+32)
            mm(P[4+h][:,:].rearrange("p (b j) -> p b j",b=GB),s.Ib[:,:],s.mkb[:,:].unsqueeze(1).broadcast_to([N,GB,N]))
            for b in range(GB): i=mm(P[4+h][:,b*N:(b+1)*N],s.qb[r,b*N:(b+1)*N],s.kb[r,b*N:(b+1)*N],start=False,stop=True,skip_group_check=True)
            i.then_inc(ev('o_s'),1)
        t.wait_ge(ev('o_vb'),g+1)
        for h in range(4):
            t.wait_ge(ev('o_e'),4*g+h+1)
            for b in range(GB): i=t.transpose(P[1+h%2][:,b*N:(b+1)*N],s.ee[h][:,b*N:(b+1)*N],I[:,:])
            i.then_inc(ev('o_pt'),1)
            if h:
                s.pv(t,mm,g,h-1)
        s.pv(t,mm,g,3)
  def pv(s,t,mm,g,h):
    t.wait_ge(s.ev('o_ptc'),4*g+h+1)
    O=s.P[3 if h<2 else 0]
    for b in range(GB):
        o=((h%2)*GB+b)*33
        i=mm(O[:,o:o+33],s.pT[h%2][:,b*N:(b+1)*N],s.vx[0][:,b,h,:])
    if h%2: i.then_inc(s.ev('o_pv'),1)

NAMES=['x','adj','L0_gnn_W1','L0_gnn_b1','L0_gnn_W2','L0_gnn_b2','L1_gnn_W1','L1_gnn_b1','L1_gnn_g1','L1_gnn_be1','L1_gnn_W2','L1_gnn_b2','L1_gnn_g2','L1_gnn_be2','L2_gnn_Wg0','L2_gnn_bg0','L2_gnn_Wg1','L2_gnn_bg1','L2_gnn_Wih','L2_gnn_Whh','L2_gnn_bih','L2_gnn_bhh','L3_gnn_W']

def kernel(**inputs):
    import numpy as _np
    import concourse.bacc as _bacc
    from concourse import mybir as _mybir
    from concourse.bass_utils import run_bass_kernel_spmd as _run
    nc = _bacc.Bacc("TRN2", target_bir_lowering=False, num_devices=1)
    arrays, args = {}, {}
    for name in NAMES:
        a = _np.ascontiguousarray(inputs[name])
        arrays[f"in_{name}_dram"] = a
        args[name] = nc.dram_tensor(f"in_{name}_dram", a.shape, _mybir.dt.from_np(a.dtype), kind="ExternalInput").ap()
    args["out"] = nc.dram_tensor("out_0_dram", (64, 128, 128), _mybir.dt.float32, kind="ExternalOutput").ap()
    build(nc, args, {}, Net)
    r = _run(nc, [arrays], core_ids=[0])
    return r.results[0]["out_0_dram"]
```

```python
import numpy as np, concourse.bass as bass
from concourse import mybir
from contextlib import ExitStack
F=mybir.dt.float32
ALU=mybir.AluOpType
ACT=mybir.ActivationFunctionType
AX=mybir.AxisListType
N=128
K=N-2
W=64
HN=N//2
HH_UNROLL=6
SEG=8
NSEG=HN//SEG
LEAF=16
SWEEPS=16
PASSES=3
EPS=2.0**-24

class Chain:
    def __init__(self, eng, sem):
        self.eng, self.sem, self.n, self.dyn = eng, sem, 0, 0
    def mark(self, ins):
        ins.then_inc(self.sem, 1)
        self.n += 1
        return self.n + self.dyn
    def wait(self, value): self.eng.wait_ge(self.sem, value)
    def __call__(self, ins):
        self.wait(self.mark(ins))
    def loop(self, i, per): self.start, self.per, self.dyn = self.n, per, i*per
    def end(self, count):
        assert self.n-self.start==self.per,(self.n-self.start,self.per)
        self.n=self.start+self.per*count
        self.dyn=0

def build(nc, ins):
  with ExitStack() as ctx:
    sb=lambda n,s,d=F: ctx.enter_context(nc.sbuf_tensor(n,s,d))
    sem=lambda n: ctx.enter_context(nc.semaphore(n))
    adj=sb("adj",[N,N])
    I=sb("I",[N,N])
    below=sb("below",[N,N])
    super_mask=sb("super_mask",[N,N])
    ones=sb("ones",[N,N])
    IOTA=sb("IOTA",[1,16])
    section=sb("section",[N,W])
    section_int=sb("section_int",[N,W],mybir.dt.int32)
    adjT=sb("adjT",[N,N])
    AhT=sb("AhT",[N,N])
    deg=sb("deg",[N,32])
    scale_diag=sb("scale_diag",[N,2*N])
    Ap=sb("Ap",[N,N])
    tmp=sb("tmp",[N,N])
    B=sb("B",[N,N])
    xcol=sb("xcol",[N,1])
    arena1=sb("arena1",[N,16384])
    arena2=sb("arena2",[N,8192])
    reflector_store=arena1[0:1,0:N*K]
    b_row=sb("b_row",[1,N])
    bcol=sb("bcol",[N,1])
    Bk=[B,sb("B1",[N,N])]
    v_rows=[sb(f"v_rows{q}",[1,N]) for q in range(2)]
    Bv_row=sb("Bv_row",[1,N])
    w_row=sb("w_row",[1,N])
    v_row=sb("v_row",[1,N])
    unused_row=sb("unused_row",[1,N])
    scal=sb("scal",[1,32])
    refl=sb("refl",[N,N])
    refl_T=sb("refl_T",[N,N])
    M1=sb("M1",[N,N])
    N1=sb("N1",[N,N])
    M2=sb("M2",[N,N])
    N2=sb("N2",[N,N])
    Z=sb("Z",[N,N])
    QT=sb("QT",[N,N])
    diag=sb("diag",[N,N])
    off=sb("off",[N,N])
    neg_off2=sb("neg_off2",[N,N])
    wide=sb("wide",[N,2*N])
    leaf_x=sb("leaf_x",[1,16])
    leaf_gamma=sb("leaf_gamma",[1,16])
    leaf_tmp=sb("leaf_tmp",[1,4])
    leaf_rp=sb("leaf_rp",[1,32])
    leaf_rp_inv=sb("leaf_rp_inv",[1,32])
    w0=sb("w0",[1,16])
    leaf_e2=sb("leaf_e2",[1,16])
    leaf_d=sb("leaf_d",[1,16])
    leaf_work=sb("leaf_work",[1,64])
    leaf=sb("leaf",[1,16])
    lam=sb("lam",[N,W])
    lo=sb("lo",[N,1])
    width=sb("width",[N,1])
    probe=sb("probe",[N,W])
    ra=sb("ra",[N,W])
    cnt=sb("cnt",[N,W])
    col=sb("col",[N,8])
    order=sb("order",[N,1])
    order_int=sb("order_int",[N,1],mybir.dt.int32)
    pair_state=sb("pair_state",[N,8])
    Y=sb("Y",[N,N])
    Y_work=sb("Y_work",[N,N])
    bound_u=sb("bound_u",[N,7])
    bound_weight=sb("bound_weight",[N,7])
    gate=sb("gate",[N,7])
    block_mass=sb("block_mass",[N,16])
    sign=sb("sign",[N,16])
    Yt=sb("Yt",[N,N])
    X=sb("X",[N,N])
    XT=sb("XT",[N,N])
    U=sb("U",[N,N])
    UT=sb("UT",[N,N])
    A_X=sb("A_X",[N,N])
    diag_pairs,off2_pairs,seq_a,seq_b,seq_c,seq_d,D_down,D_up,inv_down,inv_up,G,choice=(arena1[:,16384-(q+1)*N:16384-q*N] for q in range(12))
    P=[ctx.enter_context(nc.psum_tensor(f"P{i}",[128,512],F)) for i in range(8)]
    S={}
    def ev(n):
        if n not in S: S[n]=sem(n)
        return S[n]
    net=Net(nc,ins,sb,ev,P,(arena1,arena2,U,UT,adjT,AhT,deg,I,ones,adj))
    block=ctx.enter_context(nc.Block())
    @block.sync
    def _(eng):
        eng.dma_start(adj[:,:],ins['adj']).then_inc(ev('adj_in'),16)
        net.sync_load(eng)
        eng.wait_ge(ev('reflector_stored'),K+2)
        eng.wait_ge(ev('reflectors_zeroed'),1)
        eng.dma_start(refl[0:K,:],reflector_store.rearrange("a (k n) -> a k n",n=N)).then_inc(ev('reflectors_in'),16)
        net.sync_store(eng)
    @block.gpsimd
    def _(eng):
        c=Chain(eng,ev('gpsimd_step'))
        c.mark(eng.memset(I[:,:],0.0))
        c.mark(eng.memset(below[:,:],1.0))
        c(eng.memset(super_mask[:,:],0.0))
        eng.iota(section_int[:,:],pattern=[[1,W]],base=1,channel_multiplier=0).then_inc(ev('iota'),1)
        eng.iota(order_int[:,:],pattern=[[1,1]],base=0,channel_multiplier=1).then_inc(ev('iota'),1)
        eng.affine_select(out=I[:,:],in_=I[:,:],compare_op=ALU.not_equal,fill=1.0,base=0,pattern=[[-1,N]],channel_multiplier=1).then_inc(ev('masks'),1)
        eng.affine_select(out=below[:,:],in_=below[:,:],compare_op=ALU.is_gt,fill=0.0,base=0,pattern=[[-1,N]],channel_multiplier=1).then_inc(ev('masks'),1)
        eng.affine_select(out=super_mask[:,:],in_=super_mask[:,:],compare_op=ALU.not_equal,fill=1.0,base=1,pattern=[[-1,N]],channel_multiplier=1).then_inc(ev('masks'),1)
        eng.memset(refl[:,:],0.0).then_inc(ev('reflectors_zeroed'),1)
        eng.sem_inc(ev('reflector_stored'),2)
        eng.wait_ge(ev('masks'),3)
        with eng.Fori(0,K//HH_UNROLL) as it:
            for j in range(HH_UNROLL):
                k=it*HH_UNROLL+j
                eng.wait_ge(ev('w_row'),k+1)
                eng.tensor_copy(reflector_store[0:1,bass.ds(k*N,N)],v_rows[j%2][:,:]).then_inc(ev('reflector_stored'),1)
        with eng.Fori(0,PASSES) as s_:
            for g in range(NSEG):
                q0=(SEG+2)*g
                eng.wait_ge(ev('signs'),NSEG*s_+g+1)
                eng.tensor_tensor(arena2[:,g*SEG*2*W:(g+1)*SEG*2*W],arena1[:,q0*2*W:(q0+SEG)*2*W],arena1[:,(q0+1)*2*W:(q0+SEG+1)*2*W],ALU.mult).then_inc(ev('sign_changes'),1)
    @block.vector
    def _(v):
        c=Chain(v,ev('vector_step'))
        ts,tt,stt=v.tensor_scalar,v.tensor_tensor,v.scalar_tensor_tensor
        def ttr(o,a,b,acc,op0=ALU.mult,op1=ALU.add): return v.tensor_tensor_reduce(out=o,in0=a,in1=b,scale=1.0,scalar=0.0,op0=op0,op1=op1,accum_out=acc)
        v.memset(ones[:,:],1.0).then_inc(ev('ones'),1)
        v.wait_ge(ev('iota'),2)
        c(v.tensor_copy(section[:,:],section_int[:,:]))
        c(v.tensor_copy(order[:,:],order_int[:,:]))
        v.wait_ge(ev('adj_in'),16)
        v.wait_ge(ev('masks'),3)
        c(ttr(tmp[:,:],adj[:,:],I[:,:],deg[:,0:1]))
        c(v.tensor_reduce(deg[:,1:2],adj[:,:],AX.X,ALU.add))
        c(tt(deg[:,2:3],deg[:,1:2],deg[:,0:1],ALU.subtract))
        v.wait_ge(ev('degree_sums'),2)
        c(v.tensor_copy(adjT[:,:],P[0][:,0:N]))
        c(tt(deg[:,3:4],deg[:,2:3],P[1][:,0:1],ALU.add))
        c(ts(deg[:,4:5],deg[:,3:4],1e-30,None,ALU.max))
        c(ts(deg[:,5:6],deg[:,3:4],1.0,None,ALU.add))
        c(ts(deg[:,16:17],deg[:,3:4],0.0,None,ALU.is_gt))
        v.wait_ge(ev('degree_roots'),1)
        c(v.reciprocal(deg[:,8:10],deg[:,6:8]))
        c(tt(deg[:,10:12],deg[:,4:6],deg[:,8:10],ALU.mult))
        c(tt(deg[:,10:12],deg[:,10:12],deg[:,6:8],ALU.add))
        c(ts(deg[:,10:12],deg[:,10:12],0.5,None,ALU.mult))
        c(v.reciprocal(deg[:,12:14],deg[:,10:12]))
        c(tt(deg[:,12:13],deg[:,12:13],deg[:,16:17],ALU.mult))
        c(ts(scale_diag[:,0:N],I[:,:],deg[:,12:13],None,ALU.mult))
        ts(scale_diag[:,N:2*N],I[:,:],deg[:,13:14],None,ALU.mult).then_inc(ev('scale_diagonals'),1)
        c(tt(tmp[:,:],adj[:,:],adjT[:,:],ALU.add))
        c(ts(tmp[:,:],tmp[:,:],deg[:,12:13],-0.5,ALU.mult,ALU.mult))
        c(ts(deg[:,14:15],deg[:,3:4],deg[:,12:13],deg[:,12:13],ALU.mult,ALU.mult))
        c(ts(deg[:,15:16],deg[:,14:15],-1.0,None,ALU.add))
        v.wait_ge(ev('scale_rows'),1)
        c(tt(tmp[:,:],tmp[:,:],P[2][:,0:N],ALU.mult))
        c(stt(Ap[:,:],I[:,:],deg[:,15:16],tmp[:,:],ALU.mult,ALU.add))
        c(v.tensor_copy(B[:,:],Ap[:,:]))
        c(tt(tmp[:,:],adjT[:,:],I[:,:],ALU.add))
        c(ts(tmp[:,:],tmp[:,:],deg[:,13:14],None,ALU.mult))
        c(tt(AhT[:,:],tmp[:,:],P[2][:,N:2*N],ALU.mult))
        ts(xcol[:,:],B[:,0:1],below[:,0:1],None,ALU.mult).then_inc(ev('column'),1)
        v.tensor_copy(bcol[:,:],B[:,1:2]).then_inc(ev('next_column'),1)
        v.sem_inc(ev('B_updated'),1)
        with v.Fori(0,K//HH_UNROLL) as it:
            c.loop(it,10*HH_UNROLL)
            for j in range(HH_UNROLL):
                k=it*HH_UNROLL+j
                row=v_rows[j%2]
                nn=P[4][0:1,0:1]
                x0=P[5][0:1,0:1]
                Bo,Bn=Bk[j%2],Bk[(j+1)%2]
                v.wait_ge(ev('column_norm2'),k+1)
                twice_sign=c.mark(ts(scal[:,0:1],x0,0.0,2.0,ALU.is_ge,ALU.mult))
                v.wait_ge(ev('column_norm'),k+1)
                c.wait(twice_sign)
                sr=c.mark(ts(scal[:,1:2],scal[:,0:1],-1.0,scal[:,9:10],ALU.add,ALU.mult))
                v.wait_ge(ev('row_x'),k+1)
                v.wait_ge(ev('reflector_stored'),k+1)
                cp=c.mark(v.tensor_copy(row[:,:],P[0][0:1,0:N]))
                c.wait(sr)
                h=c.mark(ts(scal[:,2:3],x0,scal[:,1:2],nn,ALU.mult,ALU.add))
                al=row[0:1,bass.ds(k+1,1)]
                c.wait(cp)
                f=c.mark(tt(al,al,scal[:,1:2],ALU.add))
                v.wait_ge(ev('row_xB'),k+1)
                v.wait_ge(ev('row_b'),k+1)
                p=c.mark(stt(Bv_row[:,:],b_row[:,:],scal[:,1:2],P[1][0:1,0:N],ALU.mult,ALU.add))
                c.wait(h)
                hm=c.mark(ts(scal[:,4:5],scal[:,2:3],1e-30,None,ALU.max))
                c.wait(hm)
                ih=c.mark(v.reciprocal(scal[:,10:11],scal[:,4:5]))
                c.wait(p)
                vp=c.mark(ttr(unused_row[:,:],row[:,:],Bv_row[:,:],scal[:,5:6]))
                c.wait(ih)
                ts(v_row[:,:],row[:,:],scal[:,10:11],None,ALU.mult).then_inc(ev('v_scaled'),1)
                c.wait(vp)
                g=c.mark(ts(scal[:,6:7],scal[:,5:6],scal[:,10:11],-1.0,ALU.mult,ALU.mult))
                c.wait(g)
                stt(w_row[:,:],row[:,:],scal[:,6:7],Bv_row[:,:],ALU.mult,ALU.add).then_inc(ev('w_row'),1)
                v.wait_ge(ev('outer_products'),k+1)
                v.wait_ge(ev('B_updated'),k+1)
                stt(xcol[:,:],Bo[:,bass.ds(k+1,1)],P[3][:,bass.ds(k+1,1)],below[:,bass.ds(k+1,1)],ALU.subtract,ALU.mult).then_inc(ev('column'),1)
                tt(bcol[:,:],Bo[:,bass.ds(k+2,1)],P[3][:,bass.ds(k+2,1)],ALU.subtract).then_inc(ev('next_column'),1)
                tt(Bn[:,:],Bo[:,:],P[3][:,0:N],ALU.subtract).then_inc(ev('B_updated'),1)
        c.end(K//HH_UNROLL)
        v.wait_ge(ev('B_updated'),K+1)
        c(tt(wide[:,0:N],B[:,:],I[:,:],ALU.mult))
        tt(wide[:,N:2*N],B[:,:],super_mask[:,:],ALU.mult).then_inc(ev('tridiagonal_cut'),1)
        v.wait_ge(ev('tridiagonal_rows'),1)
        c(v.tensor_copy(diag[:,:],P[2][:,0:N]))
        c(v.tensor_copy(off[:,:],P[2][:,N:2*N]))
        c(stt(neg_off2[:,:],off[:,:],-1.0,off[:,:],ALU.mult,ALU.mult))
        c(ts(neg_off2[:,:],neg_off2[:,:],-1e-30,None,ALU.add))
        c(ts(leaf_d[:,:],diag[0:1,0:16],1.0,None,ALU.add))
        c(stt(leaf_work[:,0:1],off[0:1,16:17],-1.0,off[0:1,16:17],ALU.mult,ALU.max))
        c(tt(leaf_d[:,15:16],leaf_d[:,15:16],leaf_work[:,0:1],ALU.subtract))
        c(ts(leaf_e2[:,0:15],neg_off2[0:1,1:16],-1.0,None,ALU.mult))
        c(v.memset(leaf[:,:],1.0))
        with v.Fori(0,SWEEPS) as s_:
            STEPS=150
            c.loop(s_,STEPS)
            c(tt(leaf_work[:,0:15],leaf_d[:,0:15],leaf_d[:,1:16],ALU.mult))
            c(ts(leaf_work[:,16:31],leaf_work[:,0:15],-EPS*EPS,None,ALU.mult))
            c(stt(leaf_work[:,0:15],leaf_work[:,0:15],EPS*EPS,leaf_work[:,16:31],ALU.mult,ALU.max))
            c(tt(leaf_work[:,16:31],leaf_e2[:,0:15],leaf_work[:,0:15],ALU.is_gt))
            c.mark(tt(leaf_e2[:,0:15],leaf_e2[:,0:15],leaf_work[:,16:31],ALU.mult))
            c(tt(leaf_work[:,0:15],section[0:1,0:15],leaf_work[:,16:31],ALU.mult))
            c(v.tensor_reduce(leaf[:,1:2],leaf_work[:,0:15],AX.X,ALU.max))
            c(ts(leaf_work[:,16:31],section[0:1,0:15],leaf[:,1:2],None,ALU.is_equal))
            a=c.mark(ttr(leaf_work[:,0:15],leaf_work[:,16:31],leaf_d[:,1:16],leaf[:,2:3]))
            b=c.mark(ttr(leaf_work[:,32:47],leaf_work[:,16:31],leaf_d[:,0:15],leaf[:,3:4]))
            d=c.mark(ttr(leaf_work[:,48:63],leaf_work[:,16:31],leaf_e2[:,0:15],leaf[:,4:5]))
            f=c.mark(ts(leaf[:,15:16],leaf[:,1:2],0.5,None,ALU.is_ge))
            c.wait(b)
            c(ts(leaf[:,5:6],leaf[:,3:4],leaf[:,2:3],0.5,ALU.subtract,ALU.mult))
            stt(leaf[:,6:7],leaf[:,5:6],leaf[:,5:6],leaf[:,4:5],ALU.mult,ALU.add).then_inc(ev('shift_radicand'),1)
            c(ts(leaf[:,7:8],leaf[:,5:6],0.0,2.0,ALU.is_ge,ALU.mult))
            v.wait_ge(ev('shift_root'),s_+1)
            c(ts(leaf[:,8:9],leaf[:,7:8],-1.0,leaf[:,9:10],ALU.add,ALU.mult))
            c(ts(leaf[:,8:9],leaf[:,8:9],leaf[:,5:6],1e-30,ALU.add,ALU.add))
            c(v.reciprocal(leaf[:,10:11],leaf[:,8:9]))
            c(tt(leaf[:,10:11],leaf[:,10:11],leaf[:,4:5],ALU.mult))
            c(tt(leaf[:,11:12],leaf[:,2:3],leaf[:,10:11],ALU.subtract))
            c(ts(leaf_x[:,:],leaf_d[:,:],leaf[:,11:12],None,ALU.subtract))
            PRv=lambda i,n=2: leaf_rp[:,2*i:2*i+n]
            a=c.mark(ts(leaf_gamma[:,0:1],leaf_x[:,0:1],1e-17,None,ALU.add))
            c(ts(leaf[:,7:8],leaf_x[:,0:1],0.0,-2.0,ALU.is_ge,ALU.mult))
            b=c.mark(tt(PRv(0)[:,1:2],leaf_gamma[:,0:1],leaf_gamma[:,0:1],ALU.mult))
            c(tt(leaf[:,7:8],leaf[:,7:8],leaf[:,15:16],ALU.mult))
            f=c.mark(stt(leaf[:,0:1],leaf[:,7:8],1.0,leaf[:,0:1],ALU.add,ALU.mult))
            for i in range(15):
                r_,p_=leaf_rp[:,2*i:2*i+1],leaf_rp[:,2*i+1:2*i+2]
                ri,pi=leaf_rp_inv[:,2*i:2*i+1],leaf_rp_inv[:,2*i+1:2*i+2]
                pn=leaf_rp[:,2*i+3:2*i+4] if i<14 else leaf_rp[:,2*i+2:2*i+3]
                bb=leaf_e2[:,i:i+1]
                r=c.mark(tt(r_,p_,bb,ALU.add))
                x=c.mark(tt(leaf_tmp[:,0:1],leaf_x[:,i+1:i+2],p_,ALU.mult))
                t=c.mark(tt(leaf_tmp[:,1:2],bb,leaf_gamma[:,i:i+1],ALU.mult))
                c.wait(r)
                q=c.mark(v.reciprocal(leaf_rp_inv[:,2*i:2*i+2],leaf_rp[:,2*i:2*i+2]))
                c.wait(t)
                n=c.mark(tt(leaf_tmp[:,2:3],leaf_tmp[:,0:1],leaf_tmp[:,1:2],ALU.subtract))
                c.wait(q)
                u=c.mark(tt(leaf_tmp[:,3:4],r_,pi,ALU.mult))
                c.wait(n)
                c(ts(leaf_gamma[:,i+1:i+2],leaf_tmp[:,2:3],ri,1e-17,ALU.mult,ALU.add))
                c(stt(pn,leaf_gamma[:,i+1:i+2],leaf_gamma[:,i+1:i+2],leaf_tmp[:,3:4],ALU.mult,ALU.mult))
            c(tt(leaf_work[:,0:15],leaf_e2[:,0:15],leaf_rp_inv[:,0:30:2],ALU.mult))
            c.mark(tt(leaf_e2[:,0:15],leaf_work[:,0:15],leaf_rp[:,2:32:2],ALU.mult))
            c(tt(leaf_work[:,16:31],leaf_gamma[:,0:15],leaf_gamma[:,1:16],ALU.subtract))
            c(tt(leaf_d[:,0:15],leaf_d[:,1:16],leaf_work[:,16:31],ALU.add))
            c(tt(leaf_d[:,15:16],leaf[:,11:12],leaf_gamma[:,15:16],ALU.add))
        c.end(SWEEPS)
        ab=wide
        c(stt(ab[:,0:N],off[:,:],-1.0,off[:,:],ALU.mult,ALU.max))
        c(tt(ab[:,N:2*N-1],ab[:,0:N-1],ab[:,1:N],ALU.add))
        c(v.tensor_copy(ab[:,2*N-1:2*N],ab[:,N-1:N]))
        c(tt(ab[:,0:N],diag[:,:],ab[:,N:2*N],ALU.add))
        c(v.tensor_reduce(col[:,0:1],ab[:,0:N],AX.X,ALU.max))
        c(tt(ab[:,0:N],diag[:,:],ab[:,N:2*N],ALU.subtract))
        c(v.tensor_reduce(col[:,1:2],ab[:,0:N],AX.X,ALU.min))
        c(ts(col[:,0:1],col[:,0:1],1e-5,None,ALU.add))
        c(ts(lo[:,:],col[:,1:2],-1e-5,None,ALU.add))
        c(ts(width[:,:],col[:,0:1],lo[:,:],1.0/(W+1),ALU.subtract,ALU.mult))
        v.wait_ge(ev('reflectors_in'),16)
        c(ts(col[:,4:5],width[:,:],float((W+1)/8),None,ALU.mult))
        c(v.reciprocal(col[:,4:5],col[:,4:5]))
        kap=col[:,4:5]
        TD3=diag_pairs[:,:].rearrange("p (i t) -> p i t",t=2)
        NE3=off2_pairs[:,:].rearrange("p (i t) -> p i t",t=2)
        c(ts(TD3[:,:,0],diag[:,0:HN],kap,None,ALU.mult))
        c(ts(TD3[:,:,1],diag[:,N-1:HN-1:-1],kap,None,ALU.mult))
        c(v.memset(off2_pairs[:,0:2],0.0))
        c(ts(NE3[:,1:HN,0],neg_off2[:,1:HN],kap,kap,ALU.mult,ALU.mult))
        c(ts(NE3[:,1:HN,1],neg_off2[:,N-1:HN:-1],kap,kap,ALU.mult,ALU.mult))
        c(ts(col[:,5:6],neg_off2[:,HN:HN+1],kap,kap,ALU.mult,ALU.mult))
        D2=arena2[:,0:HN*2*W]
        slotS=lambda q: arena1[:,q*2*W:(q+1)*2*W]
        two=lambda t: t.rearrange("p (t w) -> p t w",t=2)
        with v.Fori(0,PASSES) as s_:
            STEPS=250
            c.loop(s_,STEPS)
            c(ts(lam[:,:],section[:,:],width[:,:],lo[:,:],ALU.mult,ALU.add))
            c(ts(probe[:,:],lam[:,:],kap,None,ALU.mult))
            c(tt(D2.rearrange("p (x w) -> p x w",w=W), diag_pairs[:,:].unsqueeze(2).broadcast_to([N,N,W]), probe[:,:].unsqueeze(1).broadcast_to([N,N,W]), ALU.subtract))
            c.mark(v.memset(slotS(0),1.0))
            pp=c.mark(v.tensor_copy(slotS(1),D2[:,0:2*W]))
            q=1
            for i in range(1,HN):
                if i%SEG==0:
                    c.wait(pp)
                    c(stt(seq_a[:,:],slotS(q),-1.0,slotS(q),ALU.mult,ALU.max))
                    c(stt(seq_b[:,:],slotS(q-1),-1.0,slotS(q-1),ALU.mult,ALU.max))
                    c(stt(seq_a[:,:],seq_a[:,:],1e-30,seq_b[:,:],ALU.add,ALU.add))
                    c(v.reciprocal(seq_a[:,:],seq_a[:,:]))
                    c.mark(tt(slotS(q+1),slotS(q-1),seq_a[:,:],ALU.mult))
                    pp=c.mark(tt(slotS(q+2),slotS(q),seq_a[:,:],ALU.mult))
                    c.wait(pp)
                    v.sem_inc(ev("segment"),1)
                    q+=2
                if i%SEG==0 or i==1: c.wait(pp-1)
                a=c.mark(tt(two(seq_b[:,:]) if i%2 else two(seq_c[:,:]),two(slotS(q-1)),NE3[:,i,:].unsqueeze(2).broadcast_to([N,2,W]),ALU.mult))
                c.wait(pp)
                b=c.mark(tt(seq_d[:,:],slotS(q),D2[:,i*2*W:(i+1)*2*W],ALU.mult))
                c.wait(b)
                pp=c.mark(tt(slotS(q+1),seq_d[:,:],(seq_b if i%2 else seq_c)[:,:],ALU.add))
                q+=1
            c.wait(pp)
            pq,rq=slotS(q)[:,0:W],slotS(q)[:,W:2*W]
            p1,r1=slotS(q-1)[:,0:W],slotS(q-1)[:,W:2*W]
            c.mark(tt(seq_a[:,0:W],pq,rq,ALU.mult))
            c(tt(seq_a[:,W:2*W],p1,r1,ALU.mult))
            c(stt(seq_a[:,0:W],seq_a[:,W:2*W],col[:,5:6],seq_a[:,0:W],ALU.mult,ALU.add))
            c(tt(seq_a[:,W:2*W],p1,rq,ALU.mult))
            v.sem_inc(ev('segment'),1)
            c(ts(seq_a[:,0:2*W],seq_a[:,0:2*W],0.0,None,ALU.is_lt))
            c(tt(seq_b[:,0:W],seq_a[:,0:W],seq_a[:,W:2*W],ALU.not_equal))
            v.wait_ge(ev('sign_changes'),NSEG*(s_+1))
            pr4=D2.rearrange("p (x w) -> p w x",w=W)
            c(v.tensor_reduce(cnt[:,:],pr4,AX.X,ALU.add))
            c(tt(cnt[:,:],cnt[:,:],D2[:,(HN-1)*2*W:(HN-1)*2*W+W],ALU.subtract))
            c(ts(cnt[:,:],cnt[:,:],-0.5,0.5*(N-1),ALU.mult,ALU.add))
            c(tt(cnt[:,:],cnt[:,:],seq_b[:,0:W],ALU.add))
            c(ts(probe[:,:],cnt[:,:],order[:,:],None,ALU.is_le))
            c(v.tensor_reduce(col[:,2:3],probe[:,:],AX.X,ALU.add))
            c(stt(lo[:,:],col[:,2:3],width[:,:],lo[:,:],ALU.mult,ALU.add))
            c(ts(width[:,:],width[:,:],1.0/(W+1),None,ALU.mult))
        c.end(PASSES)
        c(ts(col[:,3:4],width[:,:],float(W+1),None,ALU.mult))
        c(stt(pair_state[:,0:1],col[:,3:4],0.5,lo[:,:],ALU.mult,ALU.add))
        c(tt(col[:,4:5],lo[:,:],col[:,3:4],ALU.add))
        c(ts(G[:,:],diag[:,:],pair_state[:,0:1],None,ALU.subtract))
        c.mark(v.tensor_copy(D_down[:,0:1],G[:,0:1]))
        f=c.mark(v.tensor_copy(D_up[:,N-1:N],G[:,N-1:N]))
        b=f
        for i in range(1,N):
            j=N-1-i
            c.wait(f)
            f=c.mark(v.reciprocal(inv_down[:,i-1:i],D_down[:,i-1:i]))
            c.wait(b)
            b=c.mark(v.reciprocal(inv_up[:,j+1:j+2],D_up[:,j+1:j+2]))
            c.wait(f)
            f=c.mark(ts(D_down[:,i:i+1],neg_off2[:,i:i+1],inv_down[:,i-1:i],G[:,i:i+1],ALU.mult,ALU.add))
            c.wait(b)
            b=c.mark(ts(D_up[:,j:j+1],neg_off2[:,j+1:j+2],inv_up[:,j+1:j+2],G[:,j:j+1],ALU.mult,ALU.add))
        c.wait(b)
        c(tt(G[:,:],G[:,:],D_down[:,:],ALU.subtract))
        c(tt(G[:,:],D_up[:,:],G[:,:],ALU.subtract))
        c(tt(Y_work[:,:],D_down[:,:],D_down[:,:],ALU.mult))
        c(tt(Y[:,:],D_up[:,:],D_up[:,:],ALU.mult))
        c(tt(Y_work[:,:],Y_work[:,:],Y[:,:],ALU.add))
        c(tt(Y[:,:],G[:,:],G[:,:],ALU.mult))
        c(stt(Y_work[:,:],Y_work[:,:],(8*EPS)**2,Y[:,:],ALU.mult,ALU.add))
        c(v.tensor_reduce(col[:,5:6],Y_work[:,:],AX.X,ALU.min))
        c(ts(choice[:,:],Y_work[:,:],col[:,5:6],None,ALU.is_le))
        c(ttr(Y_work[:,:],choice[:,:],G[:,:],col[:,6:7]))
        c(ts(Y_work[:,:],choice[:,:],1.0,None,ALU.subtract))
        c(tt(inv_up[:,1:N],inv_up[:,1:N],off[:,1:N],ALU.mult))
        c(tt(inv_up[:,1:N],inv_up[:,1:N],Y_work[:,1:N],ALU.mult))
        c(v.memset(inv_up[:,0:1],0.0))
        c(tt(inv_down[:,0:N-1],inv_down[:,0:N-1],off[:,1:N],ALU.mult))
        c(tt(inv_down[:,0:N-1],inv_down[:,0:N-1],Y_work[:,0:N-1],ALU.mult))
        c(v.memset(inv_down[:,N-1:N],0.0))
        c(v.tensor_tensor_scan(Y[:,:],inv_up[:,:],choice[:,:],0.0,ALU.mult,ALU.add))
        c(v.tensor_tensor_scan(Y_work[:,::-1],inv_down[:,::-1],choice[:,::-1],0.0,ALU.mult,ALU.add))
        c(tt(Y[:,:],Y[:,:],Y_work[:,:],ALU.add))
        c(tt(Y[:,:],Y[:,:],choice[:,:],ALU.subtract))
        stt_=ttr(Y_work[:,:],Y[:,:],Y[:,:],pair_state[:,2:3])
        c(stt_)
        stt_=v.tensor_copy(pair_state[:,4:5],pair_state[:,2:3])
        stt_.then_inc(ev('twist_norm2'),1)
        c(v.reciprocal(pair_state[:,3:4],pair_state[:,2:3]))
        c(ts(pair_state[:,5:6],col[:,6:7],pair_state[:,3:4],pair_state[:,0:1],ALU.mult,ALU.add))
        c(ts(pair_state[:,0:1],pair_state[:,5:6],lo[:,:],col[:,4:5],ALU.max,ALU.min))
        v.wait_ge(ev('twist_norm'),1)
        c(v.reciprocal(pair_state[:,6:7],pair_state[:,1:2]))
        c(ts(Y[:,:],Y[:,:],pair_state[:,6:7],None,ALU.mult))
        c(ts(block_mass[:,0:1],Y[:,0:1],0.0,2.0,ALU.is_ge,ALU.mult))
        c(ts(block_mass[:,0:1],block_mass[:,0:1],-1.0,None,ALU.add))
        tt(leaf[:,14:15],leaf[:,0:1],leaf[:,0:1],ALU.mult).then_inc(ev('leaf_sign'),1)
        v.wait_ge(ev('leaf_sign_everywhere'),1)
        c(ts(sign[:,0:1],block_mass[:,0:1],P[4][:,0:1],None,ALU.mult))
        c(tt(Y_work[:,:],Y[:,:],Y[:,:],ALU.mult))
        c(v.tensor_reduce(block_mass[:,0:8],Y_work[:,:].rearrange("p (a b) -> p a b",b=16),AX.X,ALU.add))
        c.mark(v.memset(gate[:,3:4],1.0))
        c.mark(v.tensor_reduce(gate[:,0:7:2],block_mass[:,0:8].rearrange("p (a b) -> p a b",b=2),AX.X,ALU.add))
        c(v.tensor_reduce(gate[:,1:6:4],block_mass[:,0:8].rearrange("p (a b) -> p a b",b=4),AX.X,ALU.add))
        c(ts(gate[:,:],gate[:,:],0.5,None,ALU.is_gt))
        c(ts(wide[:,0:N],I[:,:],pair_state[:,0:1],None,ALU.mult))
        c(tt(wide[:,N:2*N],ones[:,:],wide[:,0:N],ALU.mult))
        v.sem_inc(ev('lambda_diagonal'),1)
        v.wait_ge(ev('lambda_row'),1)
        c(v.tensor_reduce(col[:,0:1],P[5][:,0:N],AX.X,ALU.max))
        c(ts(col[:,0:1],col[:,0:1],1.0,8*EPS,ALU.add,ALU.mult))
        eb,yb,ya=off[:,16::16],Y[:,16::16],Y[:,15:127:16]
        c(ts(bound_u[:,:],eb,0.0,2.0,ALU.is_ge,ALU.mult))
        c(stt(bound_u[:,:],bound_u[:,:],-1.0,yb,ALU.add,ALU.mult))
        c(tt(bound_u[:,:],bound_u[:,:],ya,ALU.add))
        c(tt(bound_weight[:,:],bound_u[:,:],eb,ALU.mult))
        c(stt(bound_weight[:,:],bound_weight[:,:],-1.0,bound_weight[:,:],ALU.mult,ALU.max))
        c(ts(bound_weight[:,:],bound_weight[:,:],col[:,0:1],None,ALU.is_gt))
        c(tt(bound_weight[:,:],bound_weight[:,:],gate[:,:],ALU.mult))
        c(ts(bound_u[:,:],bound_u[:,:],0.0,-2.0,ALU.is_ge,ALU.mult))
        c(ts(bound_u[:,:],bound_u[:,:],1.0,None,ALU.add))
        for b in (0,2,4,6,1,5,3):
            c(ts(sign[:,1:2],bound_u[:,b:b+1],sign[:,0:1],None,ALU.subtract))
            c(stt(sign[:,0:1],sign[:,1:2],bound_weight[:,b:b+1],sign[:,0:1],ALU.mult,ALU.add))
        ts(Y[:,:],Y[:,:],sign[:,0:1],None,ALU.mult).then_inc(ev('Y_ready'),1)
        c(ttr(tmp[:,:],refl[:,:],refl[:,:],deg[:,20:21]))
        c(ts(deg[:,20:21],deg[:,20:21],0.5,1e-30,ALU.mult,ALU.max))
        v.sem_inc(ev('reflector_norm2'),1)
        v.wait_ge(ev('reflector_norm'),1)
        c(v.reciprocal(deg[:,22:23],deg[:,21:22]))
        ts(refl[:,:],refl[:,:],deg[:,22:23],None,ALU.mult).then_inc(ev('reflectors_unit'),1)
        v.wait_ge(ev('reflectors_T_psum'),1)
        v.tensor_copy(refl_T[:,:],P[0][:,0:N]).then_inc(ev('reflectors_T'),1)
        v.wait_ge(ev('gram'),1)
        c(tt(M1[:,:],P[1][:,0:N],below[:,:],ALU.mult))
        v.sem_inc(ev('M_cut'),1)
        v.wait_ge(ev('N_psum'),1)
        c(v.tensor_copy(N1[:,:],P[2][:,0:N]))
        v.sem_inc(ev('N_copied'),1)
        v.wait_ge(ev('N_times_V'),1)
        c(tt(Z[:,:],refl[:,:],P[3][:,0:N],ALU.subtract))
        M=[M1,M2]
        Nn=[N1,N2]
        v.wait_ge(ev('x_in'),64)
        for s in range(6):
            a,b=s%2,(s+1)%2
            net.input_stats(v,11*s,6)
            v.wait_ge(ev('squares'),s+1)
            c(v.tensor_copy(M[b][:,:],P[1][:,0:N]))
            c(v.tensor_copy(Nn[b][:,:],P[2][:,0:N]))
            v.sem_inc(ev('squares_copied'),1)
            net.input_stats(v,11*s+6,5)
            v.wait_ge(ev('power_times_Z'),s+1)
            c(tt(Z[:,:],Z[:,:],P[3][:,0:N],ALU.add))
            v.sem_inc(ev('Z_grown'),1)
        v.wait_ge(ev('Q_correction'),1)
        c(tt(QT[:,:],I[:,:],P[1][:,0:N],ALU.subtract))
        c(v.tensor_copy(Yt[:,:],P[0][:,0:N]))
        v.sem_inc(ev('QT_ready'),1)
        v.wait_ge(ev('X_psum'),1)
        c(v.tensor_copy(X[:,:],P[2][:,0:N]))
        v.sem_inc(ev('X_ready'),1)
        for q in range(2):
            Xn,XTn=(X,XT) if q==0 else (U,UT)
            v.wait_ge(ev('A_times_X'),q+1)
            c(v.tensor_copy(A_X[:,:],P[3][:,0:N]))
            if q==0: c(v.tensor_copy(XT[:,:],P[0][:,0:N]))
            v.sem_inc(ev('W_ready'),1)
            v.wait_ge(ev('S_and_G'),q+1)
            Sx=P[1][:,0:N]
            Gx=P[2][:,0:N]
            c(ttr(tmp[:,:],Sx,I[:,:],col[:,0:1]))
            c(ttr(tmp[:,:],Gx,I[:,:],col[:,1:2]))
            c(v.reciprocal(col[:,2:3],col[:,1:2]))
            c(ts(col[:,3:4],col[:,0:1],col[:,2:3],None,ALU.mult))
            c(ts(wide[:,0:N],I[:,:],col[:,3:4],None,ALU.mult))
            v.sem_inc(ev('rayleigh_diagonal'),1)
            c(tt(tmp[:,:],I[:,:],Gx,ALU.subtract))
            v.wait_ge(ev('rayleigh_row'),q+1)
            c(ts(Y_work[:,:],P[3][:,0:N],col[:,3:4],None,ALU.subtract))
            c(tt(G[:,:],P[3][:,0:N],tmp[:,:],ALU.mult))
            c(tt(G[:,:],G[:,:],Sx,ALU.add))
            c(tt(choice[:,:],Y_work[:,:],Y_work[:,:],ALU.mult))
            c(ts(choice[:,:],choice[:,:],4e-12,None,ALU.is_ge))
            c(ts(inv_down[:,:],choice[:,:],-1.0,1.0,ALU.mult,ALU.add))
            c(tt(Y_work[:,:],Y_work[:,:],inv_down[:,:],ALU.add))
            c(v.reciprocal(Y_work[:,:],Y_work[:,:]))
            c(tt(G[:,:],G[:,:],Y_work[:,:],ALU.mult))
            c(tt(G[:,:],G[:,:],choice[:,:],ALU.mult))
            c(tt(tmp[:,:],tmp[:,:],inv_down[:,:],ALU.mult))
            c(stt(G[:,:],tmp[:,:],0.5,G[:,:],ALU.mult,ALU.add))
            v.sem_inc(ev('correction'),1)
            v.wait_ge(ev('X_times_E'),q+1)
            c(tt(U[:,:],Xn[:,:],P[1][:,0:N],ALU.add))
            c(tt(UT[:,:],XTn[:,:],P[2][:,0:N],ALU.add))
            v.sem_inc(ev('U_ready'),1)
        net.vec_pre(v,c)
        net.vector(v,c)
    @block.scalar
    def _(a):
        a.preload_act_table(ACT.Sqrt)
        a.wait_ge(ev('vector_step'),9)
        a.activation(deg[:,6:8],deg[:,4:6],ACT.Sqrt).then_inc(ev('degree_roots'),1)
        with a.Fori(0,K//HH_UNROLL) as it:
            for j in range(HH_UNROLL):
                a.wait_ge(ev('column_norm2'),it*HH_UNROLL+j+1)
                a.activation(scal[:,9:10],P[4][0:1,0:1],ACT.Sqrt).then_inc(ev('column_norm'),1)
                a.wait_ge(ev('row_b_psum'),it*HH_UNROLL+j+1)
                a.activation(b_row[:,:],P[2][0:1,0:N],ACT.Copy).then_inc(ev('row_b'),1)
        with a.Fori(0,SWEEPS) as s_:
            a.wait_ge(ev('shift_radicand'),s_+1)
            a.activation(leaf[:,9:10],leaf[:,6:7],ACT.Sqrt).then_inc(ev('shift_root'),1)
        net.scalar_pre(a)
        with a.Fori(0,PASSES) as s_:
            for g in range(NSEG):
                a.wait_ge(ev('segment'),NSEG*s_+g+1)
                q0=(SEG+2)*g
                Rg=arena1[:,q0*2*W:(q0+SEG+1)*2*W]
                a.activation(Rg,Rg,ACT.Sign).then_inc(ev('signs'),1)
        a.wait_ge(ev('twist_norm2'),1)
        a.activation(pair_state[:,1:2],pair_state[:,4:5],ACT.Sqrt).then_inc(ev('twist_norm'),1)
        a.wait_ge(ev('reflector_norm2'),1)
        a.activation(deg[:,21:22],deg[:,20:21],ACT.Sqrt).then_inc(ev('reflector_norm'),1)
        a.wait_ge(ev('U_ready'),2)
        net.scalar(a)
    @block.tensor
    def _(t):
        def mm(o,l,r,start=True,stop=True): return t.matmul(o,lhsT=l,rhs=r,start=start,stop=stop)
        t.wait_ge(ev('masks'),3)
        t.wait_ge(ev('ones'),1)
        t.wait_ge(ev('adj_in'),16)
        t.transpose(P[0][:,0:N],adj[:,:],I[:,:]).then_inc(ev('degree_sums'),1)
        mm(P[1][:,0:1],adj[:,:],ones[:,0:1]).then_inc(ev('degree_sums'),1)
        t.wait_ge(ev('scale_diagonals'),1)
        mm(P[2][:,0:2*N],ones[:,:],scale_diag[:,:]).then_inc(ev('scale_rows'),1)
        with t.Fori(0,K//HH_UNROLL) as it:
            for j in range(HH_UNROLL):
                k=it*HH_UNROLL+j
                t.wait_ge(ev('column'),k+1)
                mm(P[4][0:1,0:1],xcol[:,:],xcol[:,:])
                mm(P[5][0:1,0:1],xcol[:,:],I[:,bass.ds(k+1,1)]).then_inc(ev('column_norm2'),1)
                t.transpose(P[0][0:1,0:N],xcol[:,:],I[:,:]).then_inc(ev('row_x'),1)
                t.wait_ge(ev('next_column'),k+1)
                t.transpose(P[2][0:1,0:N],bcol[:,:],I[:,:]).then_inc(ev('row_b_psum'),1)
                t.wait_ge(ev('B_updated'),k+1)
                mm(P[1][0:1,0:N],xcol[:,:],Bk[j%2][:,:]).then_inc(ev('row_xB'),1)
                t.wait_ge(ev('v_scaled'),k+1)
                mm(P[3][:,0:N],Bv_row[:,:],v_row[:,:],stop=False)
                t.wait_ge(ev('w_row'),k+1)
                mm(P[3][:,0:N],v_row[:,:],w_row[:,:],start=False).then_inc(ev('outer_products'),1)
        t.wait_ge(ev('tridiagonal_cut'),1)
        mm(P[2][:,0:2*N],ones[:,:],wide[:,:]).then_inc(ev('tridiagonal_rows'),1)
        net.tensor_pre(t)
        t.wait_ge(ev('lstm_weights_T'),8)
        t.wait_ge(ev('leaf_sign'),1)
        mm(P[4][:,0:1],ones[0:1,:],leaf[0:1,0:1]).then_inc(ev('leaf_sign_everywhere'),1)
        t.wait_ge(ev('lambda_diagonal'),1)
        mm(P[5][:,0:N],ones[:,:],wide[:,0:N]).then_inc(ev('lambda_row'),1)
        t.wait_ge(ev('reflectors_unit'),1)
        t.transpose(P[0][:,0:N],refl[:,:],I[:,:]).then_inc(ev('reflectors_T_psum'),1)
        t.wait_ge(ev('reflectors_T'),1)
        mm(P[1][:,0:N],refl_T[:,:],refl_T[:,:]).then_inc(ev('gram'),1)
        t.wait_ge(ev('M_cut'),1)
        t.transpose(P[2][:,0:N],M1[:,:],I[:,:]).then_inc(ev('N_psum'),1)
        mm(P[3][:,0:N],M1[:,:],refl[:,:]).then_inc(ev('N_times_V'),1)
        t.wait_ge(ev('N_copied'),1)
        M=[M1,M2]
        Nn=[N1,N2]
        for s in range(6):
            a,b=s%2,(s+1)%2
            if s: t.wait_ge(ev('Z_grown'),s)
            mm(P[1][:,0:N],Nn[a][:,:],M[a][:,:])
            mm(P[2][:,0:N],M[a][:,:],Nn[a][:,:]).then_inc(ev('squares'),1)
            t.wait_ge(ev('squares_copied'),s+1)
            mm(P[3][:,0:N],M[b][:,:],Z[:,:]).then_inc(ev('power_times_Z'),1)
        t.wait_ge(ev('Z_grown'),6)
        t.wait_ge(ev('Y_ready'),1)
        t.transpose(P[0][:,0:N],Y[:,:],I[:,:])
        mm(P[1][:,0:N],Z[:,:],refl[:,:]).then_inc(ev('Q_correction'),1)
        t.wait_ge(ev('QT_ready'),1)
        mm(P[2][:,0:N],QT[:,:],Yt[:,:]).then_inc(ev('X_psum'),1)
        for q in range(2):
            Xn,XTn=(X,XT) if q==0 else (U,UT)
            if q==0:
                t.wait_ge(ev('X_ready'),1)
                t.transpose(P[0][:,0:N],X[:,:],I[:,:])
            else: t.wait_ge(ev('U_ready'),1)
            mm(P[3][:,0:N],Ap[:,:],Xn[:,:]).then_inc(ev('A_times_X'),1)
            t.wait_ge(ev('W_ready'),q+1)
            mm(P[1][:,0:N],Xn[:,:],A_X[:,:])
            mm(P[2][:,0:N],Xn[:,:],Xn[:,:]).then_inc(ev('S_and_G'),1)
            t.wait_ge(ev('rayleigh_diagonal'),q+1)
            mm(P[3][:,0:N],ones[:,:],wide[:,0:N]).then_inc(ev('rayleigh_row'),1)
            t.wait_ge(ev('correction'),q+1)
            mm(P[1][:,0:N],XTn[:,:],G[:,:])
            mm(P[2][:,0:N],G[:,:],XTn[:,:]).then_inc(ev('X_times_E'),1)
        t.wait_ge(ev('U_ready'),2)
        net.tensor(t)


BF=mybir.dt.bfloat16
NB=64
GB=4
C=GB*N
NG=NB//GB
NP=NG//2
class Net:
  def __init__(s, nc, A, sb, ev, P, T):
    s.A,s.ev,s.P=A,ev,P
    s.R1,s.R2,s.U,s.UT,s.adjT,s.AhT,s.dg,s.I,s.ones,s.adj=T
    s.allocate(sb)
    s.rowof={}
    q=0
    for n,k in (('L0_gnn_b1',1),('L1_gnn_b1',2),('L1_gnn_g1',2),('L1_gnn_be1',2),('L1_gnn_b2',1),('L1_gnn_g2',1),('L1_gnn_be2',1),('L2_gnn_bg1',1),('bih',16),('bhh',16)):
        s.rowof[n]=q
        q+=k
  def allocate(s, sb):
    R1=s.R1
    slot=lambda i,n=C: R1[:,i*C:i*C+n]
    pair=lambda n: [sb(f"{n}{u}",[N,C]) for u in range(2)]
    s.xN=sb("xN",[N,NB*N])
    s.hb,s.zb,s.yb,s.ob,s.rb=(pair(n) for n in ("hb","zb","yb","ob","rb"))
    s.bst_all=sb("bst_all",[N,6*NB])
    s.bst2=sb("bst2",[N,2*6*NG])
    s.rsd=sb("rsd",[N,NB])
    s.nmr=sb("nmr",[N,NB])
    s.nt=sb("nt",[N,4*NB])
    s.bsc=sb("bsc",[N,4])
    s.bsh=sb("bsh",[N,4])
    s.bn=sb("bn",[N,16])
    s.bnv=sb("bnv",[N,8])
    s.mx=sb("mx",[N,16])
    s.rc=sb("rc",[N,8])
    s.W0a=sb("W0a",[N,N])
    s.W0b=sb("W0b",[N,N])
    s.W1n=sb("W1n",[N,2,N])
    s.W2n=sb("W2n",[N,2*N])
    s.W1T=sb("W1T",[N,2,N])
    s.W2T=sb("W2T",[N,2,N])
    s.Wg0=sb("Wg0",[N,N])
    s.Wg1=sb("Wg1",[N,N])
    s.Wqkv=sb("Wqkv",[N,3*N])
    s.Wn=sb("Wn",[N,4,N])
    s.WT=sb("WT",[N,32,N])
    s.NR=27
    s.BR=sb("BR",[s.NR+16,N])
    s.BC=sb("BC",[N,s.NR+16])
    s.b2bc=sb("b2bc",[N,N])
    s.bg0t=sb("bg0t",[N,N])
    s.bg1t=sb("bg1t",[N,N])
    s.bl=sb("bl",[N,16])
    s.mkb=sb("mkb",[N,N],BF)
    s.Ib=sb("Ib",[N,N],BF)
    s.cb=[slot(11+u) for u in range(2)]
    s.gt=[[slot(13+4*u+k) for k in range(4)] for u in range(2)]
    s.tcb=[slot(21+u) for u in range(2)]
    s.hp=[slot(23+u) for u in range(2)]
    s.ee=[slot(h) for h in range(4)]
    s.qb=slot(4)
    s.kb=slot(5)
    s.pT=[slot(6),slot(7)]
    s.vx=[slot(q,GB*4*33).rearrange("p (b h d) -> p b h d",b=GB,h=4) for q in (8,11)]
    s.at=slot(10,256)
  def sync_load(s, eng):
    A,ev=s.A,s.ev
    for q in range(4):
        eng.dma_start(s.xN[:,q*2048:(q+1)*2048].rearrange("n (b d) -> n b d",d=N), A['x'][q*16:(q+1)*16].rearrange("b n d -> n b d")).then_inc(ev('x_in'),16)
    for t,src in ((s.W0a[:,:],A['L0_gnn_W1']),(s.W0b[:,:],A['L0_gnn_W2']),(s.W1n[:,:,:],A['L1_gnn_W1'].rearrange("(g p) d -> p g d",p=N)),(s.W2n[:,:],A['L1_gnn_W2']),
                  (s.Wg0[:,:],A['L2_gnn_Wg0']),(s.Wg1[:,:],A['L2_gnn_Wg1']),(s.Wqkv[:,:],A['L3_gnn_W'])):
        eng.dma_start(t,src).then_inc(ev('w_in'),16)
    vec=lambda n: A[n].rearrange("(g n) -> g n",n=N)
    r=0
    s.row={}
    for n,k in (('L0_gnn_b1',1),('L1_gnn_b1',2),('L1_gnn_g1',2),('L1_gnn_be1',2),('L1_gnn_b2',1),('L1_gnn_g2',1),('L1_gnn_be2',1),('L2_gnn_bg1',1)):
        s.row[n]=r
        eng.dma_start(s.BR[r:r+k,:],vec(n)).then_inc(ev('b_in'),16)
        r+=k
    s.row['bih']=r
    eng.dma_start(s.BR[r:r+16,:],A['L2_gnn_bih'].rearrange("p (g n) -> (p g) n",n=N)).then_inc(ev('b_in'),16)
    r+=16
    s.row['bhh']=r
    eng.dma_start(s.BR[r:r+16,:],A['L2_gnn_bhh'].rearrange("p (g n) -> (p g) n",n=N)).then_inc(ev('b_in'),16)
    r+=16
    assert r==s.NR+16, r
    eng.dma_start(s.b2bc[:,:],A['L0_gnn_b2'].rearrange("(a n) -> a n",a=1).broadcast_to([N,N])).then_inc(ev('b2_in'),16)
    eng.dma_start(s.bg0t[:,:],A['L2_gnn_bg0'].rearrange("(a n) -> a n",a=1).broadcast_to([N,N])).then_inc(ev('b2_in'),16)
    for q in range(8):
        if q: eng.wait_ge(ev('lstm_weights_T_psum'),q)
        eng.dma_start(s.Wn[:,:,:],A['L2_gnn_Wih' if q%2==0 else 'L2_gnn_Whh'][q//2].rearrange("(g p) d -> p g d",p=N)).then_inc(ev('lstm_weights_in'),16)
  def sync_store(s, eng):
    ev=s.ev
    with eng.Fori(0,NG) as g:
        eng.wait_ge(ev('attention_x_done'),g+1)
        eng.dma_start(s.A['out'][bass.ds(g*GB,GB)].rearrange("b n d -> n b d"), s.xN[:,bass.ds(g*C,C)].rearrange("n (b d) -> n b d",d=N)).then_inc(ev('out'),16)
    eng.wait_ge(ev('out'),16*NG)
  def ln_stats(s,v,x,g):
    for b in range(GB):
        v.bn_stats(s.bst_all[:,bass.ds(g*GB*6+b*6,6)], x[:,bass.ds(g*C+b*N,N)]).then_inc(s.ev('layer_stats'),1)
  def rsqrt(s,v,c,var,tmp,out,k):
    pass
  def ln_final(s,v,c,k):
    ev=s.ev
    bs=s.bst_all[:,:].rearrange("p (b s) -> p b s",s=6)
    nt=s.nt
    me,mo,M2e,M2o=bs[:,:,1],bs[:,:,4],bs[:,:,2],bs[:,:,5]
    a,b_,cc,d=(nt[:,i*NB:(i+1)*NB] for i in range(4))
    v.wait_ge(ev('layer_stats'),k*NB)
    c(v.tensor_tensor(a,me,mo,ALU.add))
    c(v.tensor_tensor(b_,me,mo,ALU.subtract))
    c(v.tensor_tensor(cc,M2e,M2o,ALU.add))
    c(v.scalar_tensor_tensor(b_,b_,0.25,b_,ALU.mult,ALU.mult))
    c(v.scalar_tensor_tensor(b_,cc,1.0/N,b_,ALU.mult,ALU.add))
    v.tensor_scalar(b_,b_,1e-5,None,ALU.add).then_inc(ev('layer_variance'),1)
    v.wait_ge(ev('layer_root'),k)
    c(v.reciprocal(d,cc))
    c(v.tensor_tensor(d,d,b_,ALU.mult))
    c(v.tensor_tensor(d,d,cc,ALU.add))
    c(v.tensor_scalar(d,d,0.5,None,ALU.mult))
    c(v.reciprocal(s.rsd[:,:],d))
    v.scalar_tensor_tensor(s.nmr[:,:],a,-0.5,s.rsd[:,:],ALU.mult,ALU.mult).then_inc(ev('layer_scale'),1)
  def bn_final(s,v,c,k,stats,gamma,beta,nh,col):
    ev=s.ev
    bn=s.bn
    for h in range(nh): c(v.bn_aggr(s.bnv[:,2*h:2*h+2],stats[:,h*6*NG:(h+1)*6*NG]))
    mean=s.bnv[:,0:2*nh:2]
    var=s.bnv[:,1:2*nh:2]
    v.tensor_scalar(bn[:,0:nh],var,1e-5,None,ALU.add).then_inc(ev('batch_variance'),1)
    v.wait_ge(ev('batch_root'),k)
    c(v.reciprocal(bn[:,4:4+nh],bn[:,2:2+nh]))
    c(v.tensor_tensor(bn[:,4:4+nh],bn[:,4:4+nh],bn[:,0:nh],ALU.mult))
    c(v.tensor_tensor(bn[:,4:4+nh],bn[:,4:4+nh],bn[:,2:2+nh],ALU.add))
    c(v.tensor_scalar(bn[:,4:4+nh],bn[:,4:4+nh],0.5,None,ALU.mult))
    c(v.reciprocal(bn[:,6:6+nh],bn[:,4:4+nh]))
    c(v.tensor_tensor(s.bsc[:,col:col+nh],bn[:,6:6+nh],gamma,ALU.mult))
    c(v.tensor_tensor(bn[:,8:8+nh],mean,s.bsc[:,col:col+nh],ALU.mult))
    v.tensor_tensor(s.bsh[:,col:col+nh],beta,bn[:,8:8+nh],ALU.subtract).then_inc(ev('batch_scale'),1)
  def vec_pre(s,v,c):
    ev=s.ev
    v.tensor_copy(s.Ib[:,:],s.I[:,:]).then_inc(ev('score_mask'),1)
    v.tensor_scalar(s.mkb[:,:],s.adj[:,:],0.0,-1e30,ALU.is_equal,ALU.mult).then_inc(ev('score_mask'),1)
  def input_stats(s,v,first,count):
    for b in range(first,min(first+count,NB)):
        v.bn_stats(s.bst_all[:,b*6:b*6+6], s.xN[:,b*N:(b+1)*N]).then_inc(s.ev('layer_stats'),1)
  def bcol(s,n,k=1): r=s.rowof[n]; return s.BC[:,r:r+k]
  def vector(s,v,c):
    ev=s.ev
    tt,ts,stt=v.tensor_tensor,v.tensor_scalar,v.scalar_tensor_tensor
    P=s.P
    xN=s.xN
    R1,R2=s.R1,s.R2
    X=lambda g: xN[:,bass.ds(g*C,C)]
    b4=lambda t: t[:,:].unsqueeze(1).broadcast_to([N,GB,N])
    g4=lambda t: t.rearrange("p (b d) -> p b d",d=N)
    v.wait_ge(ev('bias_columns_psum'),1)
    v.wait_ge(ev('row_sums'),1)
    c(v.tensor_copy(s.BC[:,:],P[6][:,N:N+s.NR+16]))
    c(tt(s.bl[:,:],s.bcol('bih',16),s.bcol('bhh',16),ALU.add))
    v.wait_ge(ev('b2_in'),32)
    v.wait_ge(ev('row_sums'),1)
    c(ts(s.bg0t[:,:],s.bg0t[:,:],s.dg[:,1:2],None,ALU.mult))
    ts(s.bg1t[:,:],P[6][:,0:N],s.bcol('L2_gnn_bg1'),None,ALU.mult).then_inc(ev('biases'),1)
    v.wait_ge(ev('biases'),1)
    s.ln_final(v,c,1)
    v.sem_inc(ev('spectral_x'),2)
    def copy_z(stage,it):
        for u in range(2):
            v.wait_ge(ev(stage+'product1'),2*it+u+1)
            v.tensor_copy(s.zb[u][:,:],P[u][:,:]).then_inc(ev(stage+'mixed'),1)
    def residual_a(it,more):
        for u in range(2):
            v.wait_ge(ev('spectral_product3'),2*it+u+1)
            tt(g4(s.ob[u][:,:]),g4(P[4+u][:,:]),b4(s.b2bc),ALU.add).then_inc(ev('spectral_out'),1)
        for u in range(2):
            g=2*it+u
            v.wait_ge(ev('spectral_product4'),2*it+u+1)
            tt(X(g),X(g),P[6+u][:,:],ALU.add).then_inc(ev('spectral_x'),1)
        v.wait_ge(ev('spectral_x'),2*it+3)
        s.ln_stats(v,xN,2*it)
        if more: copy_z('spectral_',it+1)
        v.wait_ge(ev('spectral_x'),2*it+4)
        s.ln_stats(v,xN,2*it+1)
    copy_z('spectral_',0)
    with v.Fori(0,NP-1) as it: residual_a(it,True)
    residual_a(NP-1,False)
    s.ln_final(v,c,2)
    v.sem_inc(ev('expand_hidden'),2)
    def hidden_b(it,more):
        for u in range(2):
            g=2*it+u
            Hb=R1[:,bass.ds(8192+g*C,C)]
            v.wait_ge(ev('expand_product2'),2*it+u+1)
            ts(Hb,P[4+u][:,:],s.bcol('L1_gnn_b1',2)[:,1:2],None,ALU.add).then_inc(ev('expand_hidden'),1)
            v.wait_ge(ev('expand_hidden'),2*it+u+3)
            v.bn_stats(s.bst2[:,bass.ds(6*NG+g*6,6)],Hb).then_inc(ev('batch_stats'),1)
            if more and u==1: copy_z('expand_',it+1)
            v.wait_ge(ev('expand_hidden_first'),2*it+u+3)
            v.bn_stats(s.bst2[:,bass.ds(g*6,6)],R1[:,bass.ds(g*C,C)]).then_inc(ev('batch_stats'),1)
    copy_z('expand_',0)
    with v.Fori(0,NP-1) as it: hidden_b(it,True)
    hidden_b(NP-1,False)
    v.wait_ge(ev('batch_stats'),2*NG)
    s.bn_final(v,c,1,s.bst2,s.bcol('L1_gnn_g1',2),s.bcol('L1_gnn_be1',2),2,0)
    v.sem_inc(ev('contract_out'),2)
    with v.Fori(0,NP) as it:
        for u in range(2):
            g=2*it+u
            v.wait_ge(ev('contract_product'),2*it+u+3)
            ts(R2[:,bass.ds(g*C,C)],P[u][:,:],s.bcol('L1_gnn_b2'),None,ALU.add).then_inc(ev('contract_out'),1)
            v.wait_ge(ev('contract_out'),2*it+u+3)
            v.bn_stats(s.bst2[:,bass.ds(g*6,6)],R2[:,bass.ds(g*C,C)]).then_inc(ev('batch_stats'),1)
    v.wait_ge(ev('batch_stats'),3*NG)
    s.bn_final(v,c,2,s.bst2,s.bcol('L1_gnn_g2'),s.bcol('L1_gnn_be2'),1,2)
    v.sem_inc(ev('mlp_residual_x'),2)
    with v.Fori(0,NP) as it:
        for u in range(2):
            g=2*it+u
            v.wait_ge(ev('mlp_residual_product'),2*it+u+3)
            tt(X(g),X(g),P[u][:,:],ALU.add).then_inc(ev('mlp_residual_x'),1)
            v.wait_ge(ev('mlp_residual_x'),2*it+u+3)
            s.ln_stats(v,xN,g)
    s.ln_final(v,c,3)
    v.sem_inc(ev('conv_out'),2)
    with v.Fori(0,NP) as it:
        for u in range(2):
            v.wait_ge(ev('conv_product1'),2*it+u+1)
            v.tensor_copy(s.zb[u][:,:],P[u][:,:]).then_inc(ev('conv_mixed'),1)
        for u in range(2):
            v.wait_ge(ev('conv_product2'),2*it+u+1)
            tt(g4(s.yb[u][:,:]),g4(P[2+u][:,:]),b4(s.bg0t),ALU.add).then_inc(ev('conv_y'),1)
        for u in range(2):
            v.wait_ge(ev('conv_product4'),2*it+u+1)
            tt(g4(s.cb[u][:,:]),g4(P[6+u][:,:]),b4(s.bg1t),ALU.add).then_inc(ev('conv_out'),1)
    v.sem_inc(ev('lstm_hidden'),2)
    base=0
    for p in range(1,5):
        BG,nw,cols,NGp=s.lstm_shape(p)
        with v.Fori(0,NGp//2) as it:
            for st in range(p):
                for u in range(2):
                    k=base+2*(it*p+st)+u+1
                    gi,gf,gg,go=(t[:,0:cols] for t in s.gt[u])
                    cbu=s.cb[u][:,0:cols]
                    v.wait_ge(ev('lstm_gates'),k+2)
                    if st==0: tt(cbu,gi,gg,ALU.mult).then_inc(ev('lstm_cell'),1)
                    else:
                        tt(gi,gi,gg,ALU.mult).then_inc(ev('lstm_cell_parts'),1)
                        tt(cbu,cbu,gf,ALU.mult).then_inc(ev('lstm_cell_parts'),1)
                        v.wait_ge(ev('lstm_cell_parts'),s.igb[p]+4*(it*(p-1)+st-1)+2*u+2)
                        tt(cbu,cbu,gi,ALU.add).then_inc(ev('lstm_cell'),1)
                for u in range(2):
                    k=base+2*(it*p+st)+u+1
                    go=s.gt[u][3][:,0:cols]
                    tc=s.tcb[u][:,0:cols]
                    v.wait_ge(ev('lstm_tanh_cell'),k)
                    if st<p-1: tt(s.hp[u][:,0:cols],go,tc,ALU.mult).then_inc(ev('lstm_hidden'),1)
                    else: tt(s.win(2*it+u,p,st),go.rearrange("p (b w) -> p b w",w=nw),tc.rearrange("p (b w) -> p b w",w=nw),ALU.mult).then_inc(ev('lstm_hidden'),1)
        base+=NGp*p
    v.sem_inc(ev('lstm_residual_x'),2)
    with v.Fori(0,NP) as it:
        for u in range(2):
            g=2*it+u
            v.wait_ge(ev('lstm_residual_product'),2*it+u+3)
            tt(X(g),X(g),P[u][:,:],ALU.add).then_inc(ev('lstm_residual_x'),1)
            v.wait_ge(ev('lstm_residual_x'),2*it+u+3)
            s.ln_stats(v,xN,g)
    s.ln_final(v,c,4)
    for u in range(2): v.memset(s.vx[u][:,:,:,:],1.0).then_inc(ev('value_ones'),1)
    v.wait_ge(ev('value_ones'),2)
    v.sem_inc(ev('attention_half_added'),1)
    s.vector_hT(v,0)
    s.vector_hT(v,1)
    with v.Fori(0,NP-1) as it:
        for u in range(2): s.vector_attention(v,2*it+u,True)
    s.vector_attention(v,NG-2,False)
    s.vector_attention(v,NG-1,False)
  def vector_hT(s,v,g):
    v.wait_ge(s.ev('attention_hT'),g+1)
    v.tensor_copy(s.zb[0][:,:],s.P[1][:,:]).then_inc(s.ev('attention_hT_copied'),1)
  def vector_attention(s,v,g,ahead):
    ev,P,tt=s.ev,s.P,v.tensor_tensor
    g4=lambda t: t.rearrange("p (b d) -> p b d",d=N)
    for h in range(4):
        v.wait_ge(ev('attention_scores'),4*g+h+1)
        S3=g4(P[4+h][:,:])
        v.tensor_reduce(s.mx[:,h*4:h*4+4],S3,AX.X,ALU.max).then_inc(ev('attention_max'),1)
        v.wait_ge(ev('attention_max'),4*g+h+1)
        tt(g4(s.ee[h][:,:]),S3,s.mx[:,h*4:h*4+4].unsqueeze(2).broadcast_to([N,GB,N]),ALU.subtract).then_inc(ev('attention_shifted'),1)
    for h in (0,2):
        v.wait_ge(ev('attention_probs_T_psum'),4*g+h+1)
        v.tensor_copy(s.pT[0][:,:],P[1][:,:]).then_inc(ev('attention_probs_T_even'),1)
    for hh in range(2):
        if hh==1 and ahead: s.vector_hT(v,g+2)
        v.wait_ge(ev('attention_weighted_v'),2*g+hh+1)
        O=P[3 if hh==0 else 0][:,0:2*GB*33].rearrange("p (h b d) -> p h b d",h=2,b=GB)
        v.reciprocal(s.rc[:,:],P[3 if hh==0 else 0][:,32:2*GB*33:33]).then_inc(ev('attention_inverse_sums'),1)
        v.wait_ge(ev('attention_inverse_sums'),2*g+hh+1)
        at=s.at[:,:].rearrange("p (h b d) -> p h b d",h=2,b=GB)
        tt(at,O[:,:,:,0:32],s.rc[:,:].rearrange("p (h b) -> p h b",h=2).unsqueeze(3).broadcast_to([N,2,GB,32]),ALU.mult).then_inc(ev('attention_normalised'),1)
        v.wait_ge(ev('attention_normalised'),2*g+hh+1)
        xs=s.xN[:,bass.ds(g*C,C)].rearrange("p (b h d) -> p h b d",b=GB,h=4)[:,2*hh:2*hh+2]
        tt(xs,xs,at,ALU.add).then_inc(ev('attention_half_added'),1)
    v.wait_ge(ev('attention_half_added'),2*g+3)
    v.sem_inc(ev('attention_x_done'),1)
  def lstm_shape(s,p):
    BG={1:4,2:8,3:8,4:16}[p]
    nw=N//p
    return BG,nw,BG*nw,NB//BG
  igb={1:0,2:0,3:2*8*1,4:2*8*1+2*8*2}
  def win(s,g,p,st):
    BG,nw,cols,_=s.lstm_shape(p)
    return s.R2[:,bass.ds(g*BG*N,BG*N)].rearrange("p (b t) -> p b t",t=N)[:,:,st:st+(nw-1)*p+1:p]
  def act_ln(s,a,it,stage,us=(0,1)):
    for u in us:
        for b in range(GB):
            col=(2*it+u)*GB+b
            i=a.activation(s.hb[u][:,b*N:(b+1)*N],s.xN[:,bass.ds((2*it+u)*C+b*N,N)],ACT.Relu,bias=s.nmr[:,bass.ds(col,1)],scale=s.rsd[:,bass.ds(col,1)])
            if b==GB-1: i.then_inc(s.ev(stage+'h'),1)
  def act_ln_sqrt(s,a,k):
    a.wait_ge(s.ev('layer_variance'),k)
    a.activation(s.nt[:,2*NB:3*NB],s.nt[:,NB:2*NB],ACT.Sqrt).then_inc(s.ev('layer_root'),1)
    a.wait_ge(s.ev('layer_scale'),k)
  def scalar(s,a):
    ev=s.ev
    P=s.P
    R1,R2=s.R1,s.R2
    act=a.activation
    a.preload_act_table(ACT.Sqrt)
    s.act_ln_sqrt(a,1)
    a.wait_ge(ev('biases'),1)
    s.scalar_main(a)
  def scalar_pre(s,a):
    ev=s.ev
    P=s.P
    act=a.activation
    for q in range(2):
        a.wait_ge(ev('mlp_weights_T_psum'),q+1)
        act((s.W1T if q==0 else s.W2T)[:,:,:].rearrange("p g n -> p (g n)"),P[7][:,q*256:q*256+256],ACT.Copy).then_inc(ev('mlp_weights_T'),1)
    for q in range(8):
        a.wait_ge(ev('lstm_weights_T_psum'),q+1)
        act(s.WT[:,4*q:4*q+4,:].rearrange("p g n -> p (g n)"),P[4][:,:],ACT.Copy).then_inc(ev('lstm_weights_T'),1)
  def scalar_main(s,a):
    ev=s.ev
    P=s.P
    R1,R2=s.R1,s.R2
    act=a.activation
    def ahead(it,u,stage,more):
        if more:
            a.wait_ge(ev(stage+'product1'),2*it+u+1)
            s.act_ln(a,it+1,stage,(u,))
    def relu_a(it,more):
        for u in range(2):
            ahead(it,u,'spectral_',more)
            a.wait_ge(ev('spectral_product2'),2*it+u+1)
            act(s.rb[u][:,:],P[2+u][:,:],ACT.Relu,bias=s.bcol('L0_gnn_b1')).then_inc(ev('spectral_relu'),1)
    s.act_ln(a,0,'spectral_')
    with a.Fori(0,NP-1) as it: relu_a(it,True)
    relu_a(NP-1,False)
    s.act_ln_sqrt(a,2)
    a.sem_inc(ev('expand_hidden_first'),2)
    def hidden_b(it,more):
        for u in range(2):
            g=2*it+u
            ahead(it,u,'expand_',more)
            a.wait_ge(ev('expand_product2'),2*it+u+1)
            act(R1[:,bass.ds(g*C,C)],P[2+u][:,:],ACT.Identity,bias=s.bcol('L1_gnn_b1',2)[:,0:1]).then_inc(ev('expand_hidden_first'),1)
    s.act_ln(a,0,'expand_')
    with a.Fori(0,NP-1) as it: hidden_b(it,True)
    hidden_b(NP-1,False)
    a.wait_ge(ev('batch_variance'),1)
    act(s.bn[:,2:4],s.bn[:,0:2],ACT.Sqrt).then_inc(ev('batch_root'),1)
    a.wait_ge(ev('batch_scale'),1)
    with a.Fori(0,NP) as it:
        for u in range(2):
            g=2*it+u
            a.wait_ge(ev('contract_product'),2*it+u+1)
            act(s.hb[u][:,:],R1[:,bass.ds(g*C,C)],ACT.Relu,bias=s.bsh[:,0:1],scale=s.bsc[:,0:1])
            act(s.yb[u][:,:],R1[:,bass.ds(8192+g*C,C)],ACT.Relu,bias=s.bsh[:,1:2],scale=s.bsc[:,1:2]).then_inc(ev('contract_hidden'),1)
    a.wait_ge(ev('batch_variance'),2)
    act(s.bn[:,2:3],s.bn[:,0:1],ACT.Sqrt).then_inc(ev('batch_root'),1)
    a.wait_ge(ev('batch_scale'),2)
    with a.Fori(0,NP) as it:
        for u in range(2):
            g=2*it+u
            a.wait_ge(ev('mlp_residual_product'),2*it+u+1)
            act(s.zb[u][:,:],R2[:,bass.ds(g*C,C)],ACT.Identity,bias=s.bsh[:,2:3],scale=s.bsc[:,2:3]).then_inc(ev('mlp_residual_mixed'),1)
    s.act_ln_sqrt(a,3)
    def layer_e(it,more):
        for u in range(2):
            ahead(it,u,'conv_',more)
            a.wait_ge(ev('conv_y'),2*it+u+1)
            act(s.rb[u][:,:],s.yb[u][:,:],ACT.Relu).then_inc(ev('conv_relu'),1)
        for u in range(2):
            a.wait_ge(ev('conv_product3'),2*it+u+1)
            act(s.ob[u][:,:],P[4+u][:,:],ACT.Copy).then_inc(ev('conv_copied'),1)
        for u in range(2):
            g=2*it+u
            a.wait_ge(ev('conv_out'),2*it+u+3)
            act(R2[:,bass.ds(g*C,C)],s.cb[u][:,:],ACT.Relu).then_inc(ev('conv_gcn'),1)
    s.act_ln(a,0,'conv_')
    with a.Fori(0,NP-1) as it: layer_e(it,True)
    layer_e(NP-1,False)
    a.preload_act_table(ACT.Sigmoid)
    a.sem_inc(ev('lstm_gates'),2)
    base=0
    for p in range(1,5):
        BG,nw,cols,NGp=s.lstm_shape(p)
        with a.Fori(0,NGp//2) as it:
            for st in range(p):
                for u in range(2):
                    k=base+2*(it*p+st)+u+1
                    a.wait_ge(ev('lstm_gate_sums'),k)
                    a.wait_ge(ev('lstm_hidden'),k)
                    for gate,f in ((0,ACT.Sigmoid),(2,ACT.Tanh))+(((1,ACT.Sigmoid),) if st else ())+((3,ACT.Sigmoid),):
                        i=act(s.gt[u][gate][:,0:cols],P[4*u+gate][:,0:cols],f,bias=s.bl[:,4*(p-1)+gate:4*(p-1)+gate+1])
                    i.then_inc(ev('lstm_gates'),1)
                for u in range(2):
                    k=base+2*(it*p+st)+u+1
                    a.wait_ge(ev('lstm_cell'),k)
                    act(s.tcb[u][:,0:cols],s.cb[u][:,0:cols],ACT.Tanh).then_inc(ev('lstm_tanh_cell'),1)
        base+=NGp*p
    a.preload_act_table(ACT.Sqrt)
    a.wait_ge(ev('lstm_hidden'),base+2)
    with a.Fori(0,NP) as it:
        for u in range(2):
            a.wait_ge(ev('lstm_residual_product'),2*it+u+1)
            act(s.zb[u][:,:],R2[:,bass.ds((2*it+u)*C,C)],ACT.Copy).then_inc(ev('lstm_residual_mixed'),1)
    s.act_ln_sqrt(a,4)
    a.preload_act_table(ACT.Exp)
    s.scalar_h(a,0)
    a.wait_ge(ev('value_ones'),2)
    s.scalar_q(a,0)
    s.scalar_k(a,0)
    s.scalar_v(a,0,0)
    a.wait_ge(ev('attention_hT'),1)
    s.scalar_h(a,1)
    with a.Fori(0,NP-1) as it:
        for u in range(2): s.scalar_attention(a,2*it+u,u,True,True)
    s.scalar_attention(a,NG-2,0,False,True)
    s.scalar_attention(a,NG-1,1,False,False)
  def scalar_h(s,a,g):
    for b in range(GB):
        i=a.activation(s.hb[0][:,b*N:(b+1)*N],s.xN[:,bass.ds(g*C+b*N,N)],ACT.Relu,bias=s.nmr[:,bass.ds(g*GB+b,1)],scale=s.rsd[:,bass.ds(g*GB+b,1)])
    i.then_inc(s.ev('attention_h'),1)
  def scalar_q(s,a,g):
    a.wait_ge(s.ev('attention_q_psum'),g+1)
    a.activation(s.qb[:,:],s.P[1][:,:],ACT.Copy,scale=float(32**-0.5)).then_inc(s.ev('attention_q'),1)
  def scalar_k(s,a,g):
    a.wait_ge(s.ev('attention_k_psum'),g+1)
    a.activation(s.kb[:,:],s.P[2][:,:],ACT.Copy).then_inc(s.ev('attention_k'),1)
  def scalar_v(s,a,g,u):
    a.wait_ge(s.ev('attention_v_psum'),g+1)
    a.activation(s.vx[u][:,:,:,0:32],s.P[0][:,:].rearrange("p (b h d) -> p b h d",b=GB,h=4),ACT.Copy).then_inc(s.ev('attention_v'),1)
  def scalar_attention(s,a,g,u,ahead,more):
    ev=s.ev
    if ahead:
        a.wait_ge(ev('attention_hT'),g+2)
        s.scalar_h(a,g+2)
    for h in range(4):
        a.wait_ge(ev('attention_shifted'),4*g+h+1)
        a.activation(s.ee[h][:,:],s.ee[h][:,:],ACT.Exp).then_inc(ev('attention_exp'),1)
        if more and h==1: s.scalar_q(a,g+1)
        if more and h==2: s.scalar_k(a,g+1)
    if more: s.scalar_v(a,g+1,1-u)
    for h in (1,3):
        a.wait_ge(ev('attention_probs_T_psum'),4*g+h+1)
        a.activation(s.pT[1][:,:],s.P[2][:,:],ACT.Copy).then_inc(ev('attention_probs_T_odd'),1)
  def tensor_pre(s,t):
    ev=s.ev
    P=s.P
    I=s.I[:,:]
    t.wait_ge(ev('w_in'),16*7)
    for g in range(2): i=t.transpose(P[7][:,g*N:(g+1)*N],s.W1n[:,g,:],I)
    i.then_inc(ev('mlp_weights_T_psum'),1)
    t.wait_ge(ev('mlp_weights_T'),1)
    for g in range(2): i=t.transpose(P[7][:,(2+g)*N:(3+g)*N],s.W2n[:,g*N:(g+1)*N],I)
    i.then_inc(ev('mlp_weights_T_psum'),1)
    for q in range(8):
        t.wait_ge(ev('lstm_weights_in'),16*(q+1))
        if q: t.wait_ge(ev('lstm_weights_T'),q)
        for g in range(4): i=t.transpose(P[4][:,g*N:(g+1)*N],s.Wn[:,g,:],I)
        i.then_inc(ev('lstm_weights_T_psum'),1)
       
    t.wait_ge(ev('b_in'),160)
    nr=s.NR+16
    t.transpose(P[6][:,N:N+nr],s.BR[:,:],s.I[0:nr,0:nr]).then_inc(ev('bias_columns_psum'),1)
    t.matmul(P[6][:,0:N],lhsT=s.ones[:,:],rhs=s.adjT[:,:],start=True,stop=True).then_inc(ev('row_sums'),1)
  def tensor(s,t):
    ev=s.ev
    P=s.P
    I=s.I
    def mm(o,l,r,start=True,stop=True,**k): return t.matmul(o,lhsT=l,rhs=r,start=start,stop=stop,**k)
    def mix(dst,src,M):
        for b in range(GB): i=mm(dst[:,b*N:(b+1)*N],src[:,b*N:(b+1)*N],M)
        return i
    t.wait_ge(ev('mlp_weights_T'),2)
    t.wait_ge(ev('lstm_weights_T'),8)
    with t.Fori(0,NP) as it:
        for u in range(2):
            t.wait_ge(ev('spectral_h'),2*it+u+1)
            mix(P[u],s.hb[u],s.U[:,:]).then_inc(ev('spectral_product1'),1)
        for u in range(2):
            t.wait_ge(ev('spectral_mixed'),2*it+u+1)
            mm(P[2+u][:,:],s.W0a[:,:],s.zb[u][:,:]).then_inc(ev('spectral_product2'),1)
        for u in range(2):
            t.wait_ge(ev('spectral_relu'),2*it+u+1)
            mix(P[4+u],s.rb[u],s.W0b[:,:]).then_inc(ev('spectral_product3'),1)
        for u in range(2):
            t.wait_ge(ev('spectral_out'),2*it+u+1)
            t.wait_ge(ev('spectral_x'),2*it+u+1)
            mm(P[6+u][:,:],s.UT[:,:],s.ob[u][:,:]).then_inc(ev('spectral_product4'),1)
    with t.Fori(0,NP) as it:
        for u in range(2):
            t.wait_ge(ev('expand_h'),2*it+u+1)
            mix(P[u],s.hb[u],s.AhT[:,:]).then_inc(ev('expand_product1'),1)
        for u in range(2):
            t.wait_ge(ev('expand_mixed'),2*it+u+1)
            t.wait_ge(ev('expand_hidden'),2*it+u+1)
            t.wait_ge(ev('expand_hidden_first'),2*it+u+1)
            mm(P[2+u][:,:],s.W1T[:,0,:],s.zb[u][:,:])
            mm(P[4+u][:,:],s.W1T[:,1,:],s.zb[u][:,:]).then_inc(ev('expand_product2'),1)
    t.sem_inc(ev('contract_product'),2)
    with t.Fori(0,NP) as it:
        for u in range(2):
            t.wait_ge(ev('contract_hidden'),2*it+u+1)
            t.wait_ge(ev('contract_out'),2*it+u+1)
            mm(P[u][:,:],s.W2T[:,0,:],s.hb[u][:,:],stop=False)
            mm(P[u][:,:],s.W2T[:,1,:],s.yb[u][:,:],start=False).then_inc(ev('contract_product'),1)
    t.sem_inc(ev('mlp_residual_product'),2)
    with t.Fori(0,NP) as it:
        for u in range(2):
            t.wait_ge(ev('mlp_residual_mixed'),2*it+u+1)
            t.wait_ge(ev('mlp_residual_x'),2*it+u+1)
            for b in range(GB): i=t.transpose(P[u][:,b*N:(b+1)*N],s.zb[u][:,b*N:(b+1)*N],I[:,:])
            i.then_inc(ev('mlp_residual_product'),1)
    with t.Fori(0,NP) as it:
        for u in range(2):
            t.wait_ge(ev('conv_h'),2*it+u+1)
            mix(P[u],s.hb[u],s.adjT[:,:]).then_inc(ev('conv_product1'),1)
        for u in range(2):
            t.wait_ge(ev('conv_mixed'),2*it+u+1)
            mix(P[2+u],s.zb[u],s.Wg0[:,:]).then_inc(ev('conv_product2'),1)
        for u in range(2):
            t.wait_ge(ev('conv_relu'),2*it+u+1)
            mix(P[4+u],s.rb[u],s.adjT[:,:]).then_inc(ev('conv_product3'),1)
        for u in range(2):
            t.wait_ge(ev('conv_copied'),2*it+u+1)
            t.wait_ge(ev('conv_out'),2*it+u+1)
            mm(P[6+u][:,:],s.Wg1[:,:],s.ob[u][:,:]).then_inc(ev('conv_product4'),1)
    t.wait_ge(ev('conv_gcn'),NG)
    t.wait_ge(ev('conv_out'),NG+2)
    base=0
    for p in range(1,5):
        BG,nw,cols,NGp=s.lstm_shape(p)
        if base: t.wait_ge(ev('lstm_hidden'),base+2)
        with t.Fori(0,NGp//2) as it:
            for st in range(p):
                for u in range(2):
                    k=base+2*(it*p+st)+u+1
                    gates=(0,2,1,3) if st else (0,2,3)
                    t.wait_ge(ev('lstm_gates'),k)
                    xs=s.win(2*it+u,p,st)
                    for gate in gates: i=mm(P[4*u+gate][:,0:cols].rearrange("p (b w) -> p b w",w=nw),s.WT[:,(2*(p-1))*4+gate,:],xs,stop=(st==0))
                    if st:
                        t.wait_ge(ev('lstm_hidden'),k)
                        for gate in gates: i=mm(P[4*u+gate][:,0:cols],s.WT[:,(2*(p-1)+1)*4+gate,:],s.hp[u][:,0:cols],start=False)
                    i.then_inc(ev('lstm_gate_sums'),1)
        base+=NGp*p
    t.wait_ge(ev('lstm_hidden'),base+2)
    t.sem_inc(ev('lstm_residual_product'),2)
    with t.Fori(0,NP) as it:
        for u in range(2):
            g=2*it+u
            t.wait_ge(ev('lstm_residual_mixed'),2*it+u+1)
            t.wait_ge(ev('lstm_residual_x'),2*it+u+1)
            for b in range(GB): i=t.transpose(P[u][:,b*N:(b+1)*N],s.zb[u][:,b*N:(b+1)*N],I[:,:])
            i.then_inc(ev('lstm_residual_product'),1)
    t.wait_ge(ev('score_mask'),2)
    t.wait_ge(ev('lstm_residual_x'),NG+2)
    s.tensor_hT(t,0)
    s.tensor_qkv(t,0)
    t.wait_ge(ev('attention_q'),1)
    t.wait_ge(ev('attention_k'),1)
    t.wait_ge(ev('attention_v'),1)
    s.tensor_hT(t,1)
    with t.Fori(0,NP-1) as it:
        for u in range(2): s.tensor_attention(t,2*it+u,u,True,True)
    s.tensor_attention(t,NG-2,0,False,True)
    s.tensor_attention(t,NG-1,1,False,False)
  def tensor_hT(s,t,g):
    t.wait_ge(s.ev('attention_h'),g+1)
    for b in range(GB): i=t.transpose(s.P[1][:,b*N:(b+1)*N],s.hb[0][:,b*N:(b+1)*N],s.I[:,:])
    i.then_inc(s.ev('attention_hT'),1)
  def tensor_qkv(s,t,g):
    ev,P=s.ev,s.P
    def mm(o,l,r,start=True,stop=True): return t.matmul(o,lhsT=l,rhs=r,start=start,stop=stop)
    t.wait_ge(ev('attention_hT_copied'),g+1)
    mm(P[1][:,:],s.Wqkv[:,0:N],s.zb[0][:,:]).then_inc(ev('attention_q_psum'),1)
    mm(P[2][:,:],s.Wqkv[:,N:2*N],s.zb[0][:,:]).then_inc(ev('attention_k_psum'),1)
    t.wait_ge(ev('attention_half_added'),2*g-1 if not isinstance(g,int) or g else 1)
    for b in range(GB): i=mm(P[0][:,b*N:(b+1)*N],s.zb[0][:,b*N:(b+1)*N],s.Wqkv[:,2*N:3*N])
    i.then_inc(ev('attention_v_psum'),1)
  def tensor_attention(s,t,g,u,ahead,more):
    ev,P=s.ev,s.P
    def mm(o,l,r,start=True,stop=True,**k): return t.matmul(o,lhsT=l,rhs=r,start=start,stop=stop,**k)
    for h in range(4):
        r=slice(32*h,32*h+32)
        mm(P[4+h][:,:].rearrange("p (b j) -> p b j",b=GB),s.Ib[:,:],s.mkb[:,:].unsqueeze(1).broadcast_to([N,GB,N]))
        for b in range(GB): i=mm(P[4+h][:,b*N:(b+1)*N],s.qb[r,b*N:(b+1)*N],s.kb[r,b*N:(b+1)*N],start=False,stop=True,skip_group_check=True)
        i.then_inc(ev('attention_scores'),1)
    if more: s.tensor_qkv(t,g+1)
    else: t.wait_ge(ev('attention_half_added'),2*g+1)
    for h in range(4):
        t.wait_ge(ev('attention_exp'),4*g+h+1)
        if more and h==0: t.wait_ge(ev('attention_q'),g+2)
        if more and h==1: t.wait_ge(ev('attention_k'),g+2)
        for b in range(GB): i=t.transpose(P[1+h%2][:,b*N:(b+1)*N],s.ee[h][:,b*N:(b+1)*N],s.I[:,:])
        i.then_inc(ev('attention_probs_T_psum'),1)
        if more and h==3: t.wait_ge(ev('attention_v'),g+2)
        if h: s.pv(t,mm,g,u,h-1)
    if ahead: s.tensor_hT(t,g+2)
    s.pv(t,mm,g,u,3)
  def pv(s,t,mm,g,u,h):
    t.wait_ge(s.ev('attention_probs_T_odd' if h%2 else 'attention_probs_T_even'),2*g+h//2+1)
    O=s.P[3 if h<2 else 0]
    for b in range(GB):
        o=((h%2)*GB+b)*33
        i=mm(O[:,o:o+33],s.pT[h%2][:,b*N:(b+1)*N],s.vx[u][:,b,h,:])
    if h%2: i.then_inc(s.ev('attention_weighted_v'),1)


NAMES = ['x', 'adj', 'L0_gnn_W1', 'L0_gnn_b1', 'L0_gnn_W2', 'L0_gnn_b2', 'L1_gnn_W1', 'L1_gnn_b1', 'L1_gnn_g1', 'L1_gnn_be1',
         'L1_gnn_W2', 'L1_gnn_b2', 'L1_gnn_g2', 'L1_gnn_be2', 'L2_gnn_Wg0', 'L2_gnn_bg0', 'L2_gnn_Wg1', 'L2_gnn_bg1',
         'L2_gnn_Wih', 'L2_gnn_Whh', 'L2_gnn_bih', 'L2_gnn_bhh', 'L3_gnn_W']


def kernel(**inputs):
    import numpy as _np
    import concourse.bacc as _bacc
    from concourse import mybir as _mybir
    from concourse.bass_utils import run_bass_kernel_spmd as _run
    nc = _bacc.Bacc("TRN2", target_bir_lowering=False, num_devices=1)
    arrays, args = {}, {}
    for name in NAMES:
        a = _np.ascontiguousarray(inputs[name])
        arrays[f"in_{name}_dram"] = a
        args[name] = nc.dram_tensor(f"in_{name}_dram", a.shape, _mybir.dt.from_np(a.dtype), kind="ExternalInput").ap()
    args["out"] = nc.dram_tensor("out_0_dram", (64, 128, 128), _mybir.dt.float32, kind="ExternalOutput").ap()
    build(nc, args)
    r = _run(nc, [arrays], core_ids=[0])
    return r.results[0]["out_0_dram"]
```
